# Optimizing a Trainium2 kernel written in Bass

```python
import numpy as np
import jax
import jax.numpy as jnp

def _softmax(x, axis=-1):
    return jax.nn.softmax(x, axis=axis)

def _gelu(x):
    return jax.nn.gelu(x, approximate=True)

def _silu(x):
    return jax.nn.silu(x)

def _sigmoid(x):
    return jax.nn.sigmoid(x)

def _layernorm(x, axis=-1, eps=1e-05):
    m = jnp.mean(x, axis=axis, keepdims=True)
    v = jnp.var(x, axis=axis, keepdims=True)
    return (x - m) / jnp.sqrt(v + eps)

def _scatter_add(tgt, idx, src, axis=0):
    return tgt.at[idx].add(src)

def _segment_sum(src, seg, n):
    return jax.ops.segment_sum(src, seg, n)
kernel_name = 'mk_flamingo_gated_d1_seqx_r4_635fb9'

def setup_inputs(seed: int=0):
    np.random.seed(seed)
    _w = jnp.asarray

    def _rec_inputs():
        import jax
        import jax.numpy as jnp
        _rk = jax.random.key(seed)
        x = -0.0002928 + 1 * jax.random.normal(jax.random.fold_in(_rk, 1), (32, 128, 512), jnp.float32)
        _lenS = 128 - jax.random.randint(jax.random.fold_in(_rk, 7), (32,), 0, max(1, 128 // 4) + 1, jnp.int32)
        _lenS2 = 128 - jax.random.randint(jax.random.fold_in(_rk, 8), (32,), 0, max(1, 128 // 4) + 1, jnp.int32)
        _ctx_512P = jax.random.normal(jax.random.fold_in(_rk, 11), (32, 16, 128), jnp.float32)
        _ctx_512c = jax.random.dirichlet(jax.random.fold_in(_rk, 511), 0.3 * jnp.ones((16,), jnp.float32), (32, 128))
        _ctx_512t = jnp.einsum('bsk,bkd->bsd', _ctx_512c, _ctx_512P)
        _ctx_512t = _ctx_512t * jax.lax.rsqrt(jnp.mean(jnp.square(_ctx_512t)) + 1e-12) * 0.953939
        ctx_512 = 0.000227908 + 0.99994 * (_ctx_512t + 0.3 * jax.random.normal(jax.random.fold_in(_rk, 611), (32, 128, 128), jnp.float32))
        _g = jax.random.normal(jax.random.fold_in(_rk, 9001), (2, 1), jnp.float32)
        _g = jnp.sign(_g) * jnp.maximum(jnp.abs(_g), 1.0) + (_g == 0) * 1.0
        g_xattn = _g[0]
        g_ffn = _g[1]
        return (x, ctx_512, g_xattn, g_ffn)
    x, ctx_512, g_xattn, g_ffn = _rec_inputs()

    def _L0_xattn_setup():
        import jax, jax.numpy as jnp
        import numpy as np
        B, S, L = (2, 256, 256)
        DIM_Q, H, K, D_C, D_CQ, R = (512, 16, 128, 128, 384, 64)

        def _rope_tables(seq_len, dim, dtype):
            inv_freq = 1.0 / 10000.0 ** (jnp.arange(0, dim, 2, dtype=dtype) / dim)
            t = jnp.arange(seq_len, dtype=dtype)
            freqs = t[:, None] * inv_freq[None, :]
            sin = jnp.repeat(jnp.sin(freqs), 2, axis=-1)
            cos = jnp.repeat(jnp.cos(freqs), 2, axis=-1)
            return (sin, cos)

        def _rotate_half(x):
            h = x.shape[-1] // 2
            return jnp.concatenate([-x[..., h:], x[..., :h]], axis=-1)
        key = jax.random.key(seed)
        ks = jax.random.split(key, 8)
        s_in = 1.0 / np.sqrt(DIM_Q)
        s_k = 1.0 / np.sqrt(K)
        s_cq = 1.0 / np.sqrt(D_CQ)
        s_c = 1.0 / np.sqrt(D_C)
        return {'hidden_q': jax.random.normal(ks[0], (B, S, DIM_Q), jnp.float32), 'kv_c': jax.random.normal(ks[1], (B, L, D_C), jnp.float32), 'Wq': jax.random.normal(ks[2], (H * K, DIM_Q), jnp.float32) * s_in, 'w_kc_q': jax.random.normal(ks[3], (H, K, D_CQ), jnp.float32) * s_k, 'w_kc_kv': jax.random.normal(ks[4], (H, K, D_C), jnp.float32) * s_k, 'W_qr': jax.random.normal(ks[5], (H, D_CQ, R), jnp.float32) * s_cq / np.sqrt(R), 'W_kr': jax.random.normal(ks[6], (H, D_C, R), jnp.float32) * s_c, 'Wo': jax.random.normal(ks[7], (DIM_Q, H * K), jnp.float32) * s_k}
    _L0_xattn_all = _L0_xattn_setup()
    _L0_xattn_in = {k: v for k, v in _L0_xattn_all.items() if k in ('Wq', 'w_kc_q', 'w_kc_kv', 'W_qr', 'W_kr', 'Wo')}
    del _L0_xattn_all

    def _L0_ffn_setup():
        import jax, jax.numpy as jnp
        import numpy as np
        B, S, D = (4, 1024, 512)
        E, K, I, J = (8, 2, 352, 1408)
        CAP_FACTOR = 1.25
        STD = 0.02

        def _moe_routed(x_flat, router, w_up_gate, w_down):
            T, d = x_flat.shape
            logits = jnp.einsum('td,de->te', x_flat, router)
            topk_logits, sel = jax.lax.top_k(logits, K)
            cw = jax.nn.softmax(topk_logits, axis=-1).astype(x_flat.dtype)
            C = int(np.ceil(T * K / E * CAP_FACTOR))
            e_flat = sel.reshape(-1)
            oh = jax.nn.one_hot(e_flat, E, dtype=jnp.int32)
            pos_all = jnp.cumsum(oh, axis=0) - oh
            pos = jnp.take_along_axis(pos_all, e_flat[:, None], axis=1)[:, 0]
            valid = pos < C
            safe_pos = jnp.where(valid, pos, C)
            tok = jnp.repeat(jnp.arange(T), K)
            buf = jnp.zeros((E, C, d), x_flat.dtype).at[e_flat, safe_pos].set(x_flat[tok], mode='drop')
            gate_up = jnp.einsum('ecd,edm->ecm', buf, w_up_gate)
            gate, up = jnp.split(gate_up, [I], axis=-1)
            h = jax.nn.silu(gate) * up
            out_buf = jnp.einsum('eci,eid->ecd', h, w_down)
            gathered = out_buf[e_flat, jnp.minimum(safe_pos, C - 1)]
            gathered = gathered * valid[:, None].astype(x_flat.dtype)
            w = cw.reshape(-1)
            y = jnp.zeros((T, d), x_flat.dtype).at[tok].add(w[:, None] * gathered)
            return y

        def _shared_mlp(x_flat, shared_w_up_gate, shared_w_down):
            gu = jnp.einsum('td,dm->tm', x_flat, shared_w_up_gate)
            gate, up = jnp.split(gu, [J], axis=-1)
            return jnp.einsum('tm,md->td', jax.nn.silu(gate) * up, shared_w_down)
        key = jax.random.key(seed)
        kx, kr, ku, kd, ksu, ksd = jax.random.split(key, 6)
        x = jax.random.normal(kx, (B, S, D), dtype=jnp.float32)
        router = STD * jax.random.truncated_normal(kr, -3, 3, (D, E), dtype=jnp.float32)
        w_up_gate = STD * jax.random.truncated_normal(ku, -3, 3, (E, D, 2 * I), dtype=jnp.float32)
        w_down = STD * jax.random.truncated_normal(kd, -3, 3, (E, I, D), dtype=jnp.float32)
        shared_w_up_gate = STD * jax.random.truncated_normal(ksu, -3, 3, (D, 2 * J), dtype=jnp.float32)
        shared_w_down = STD * jax.random.truncated_normal(ksd, -3, 3, (J, D), dtype=jnp.float32)
        return {'x': x, 'router': router, 'w_up_gate': w_up_gate, 'w_down': w_down, 'shared_w_up_gate': shared_w_up_gate, 'shared_w_down': shared_w_down}
    _L0_ffn_all = _L0_ffn_setup()
    _L0_ffn_in = {k: v for k, v in _L0_ffn_all.items() if k in ('router', 'w_up_gate', 'w_down', 'shared_w_up_gate', 'shared_w_down')}
    del _L0_ffn_all
    return {'x': x, 'ctx_512': ctx_512, 'g_xattn': g_xattn, 'g_ffn': g_ffn, 'L0_xattn_Wq': _L0_xattn_in['Wq'], 'L0_xattn_w_kc_q': _L0_xattn_in['w_kc_q'], 'L0_xattn_w_kc_kv': _L0_xattn_in['w_kc_kv'], 'L0_xattn_W_qr': _L0_xattn_in['W_qr'], 'L0_xattn_W_kr': _L0_xattn_in['W_kr'], 'L0_xattn_Wo': _L0_xattn_in['Wo'], 'L0_ffn_router': _L0_ffn_in['router'], 'L0_ffn_w_up_gate': _L0_ffn_in['w_up_gate'], 'L0_ffn_w_down': _L0_ffn_in['w_down'], 'L0_ffn_shared_w_up_gate': _L0_ffn_in['shared_w_up_gate'], 'L0_ffn_shared_w_down': _L0_ffn_in['shared_w_down']}

def reference(x, ctx_512, g_xattn, g_ffn, L0_xattn_Wq, L0_xattn_w_kc_q, L0_xattn_w_kc_kv, L0_xattn_W_qr, L0_xattn_W_kr, L0_xattn_Wo, L0_ffn_router, L0_ffn_w_up_gate, L0_ffn_w_down, L0_ffn_shared_w_up_gate, L0_ffn_shared_w_down):
    import jax
    import jax.numpy as jnp

    def _L0_xattn_ref(hidden_q, kv_c, Wq, w_kc_q, w_kc_kv, W_qr, W_kr, Wo):
        import jax, jax.numpy as jnp
        import numpy as np
        B, S, L = (2, 256, 256)
        DIM_Q, H, K, D_C, D_CQ, R = (512, 16, 128, 128, 384, 64)

        def _rope_tables(seq_len, dim, dtype):
            inv_freq = 1.0 / 10000.0 ** (jnp.arange(0, dim, 2, dtype=dtype) / dim)
            t = jnp.arange(seq_len, dtype=dtype)
            freqs = t[:, None] * inv_freq[None, :]
            sin = jnp.repeat(jnp.sin(freqs), 2, axis=-1)
            cos = jnp.repeat(jnp.cos(freqs), 2, axis=-1)
            return (sin, cos)

        def _rotate_half(x):
            h = x.shape[-1] // 2
            return jnp.concatenate([-x[..., h:], x[..., :h]], axis=-1)
        b, s, _ = hidden_q.shape
        l = kv_c.shape[1]
        q_hk = (hidden_q @ Wq.T).reshape(b, s, H, K)
        q_big = jnp.einsum('bshk,hkq->bshq', q_hk, w_kc_q)
        sin, cos = _rope_tables(l, D_C, kv_c.dtype)
        kv_rope = kv_c * cos[None] + _rotate_half(kv_c) * sin[None]
        q_r = jnp.einsum('bshq,hqr->bhsr', q_big, W_qr)
        k_r = jnp.einsum('bld,hdr->bhlr', kv_rope, W_kr)
        scores = jnp.einsum('bhsr,bhlr->bhsl', q_r, k_r)
        attn = jax.nn.softmax(scores, axis=-1)
        ctx_c = jnp.einsum('bhsl,bld->bhsd', attn, kv_rope)
        ctx_lat = jnp.einsum('bhsd,hkd->bshk', ctx_c, w_kc_kv)
        out = ctx_lat.reshape(b, s, H * K) @ Wo.T
        return out

    def _L0_ffn_ref(x, router, w_up_gate, w_down, shared_w_up_gate, shared_w_down):
        import jax, jax.numpy as jnp
        import numpy as np
        B, S, D = (4, 1024, 512)
        E, K, I, J = (8, 2, 352, 1408)
        CAP_FACTOR = 1.25
        STD = 0.02

        def _moe_routed(x_flat, router, w_up_gate, w_down):
            T, d = x_flat.shape
            logits = jnp.einsum('td,de->te', x_flat, router)
            topk_logits, sel = jax.lax.top_k(logits, K)
            cw = jax.nn.softmax(topk_logits, axis=-1).astype(x_flat.dtype)
            C = int(np.ceil(T * K / E * CAP_FACTOR))
            e_flat = sel.reshape(-1)
            oh = jax.nn.one_hot(e_flat, E, dtype=jnp.int32)
            pos_all = jnp.cumsum(oh, axis=0) - oh
            pos = jnp.take_along_axis(pos_all, e_flat[:, None], axis=1)[:, 0]
            valid = pos < C
            safe_pos = jnp.where(valid, pos, C)
            tok = jnp.repeat(jnp.arange(T), K)
            buf = jnp.zeros((E, C, d), x_flat.dtype).at[e_flat, safe_pos].set(x_flat[tok], mode='drop')
            gate_up = jnp.einsum('ecd,edm->ecm', buf, w_up_gate)
            gate, up = jnp.split(gate_up, [I], axis=-1)
            h = jax.nn.silu(gate) * up
            out_buf = jnp.einsum('eci,eid->ecd', h, w_down)
            gathered = out_buf[e_flat, jnp.minimum(safe_pos, C - 1)]
            gathered = gathered * valid[:, None].astype(x_flat.dtype)
            w = cw.reshape(-1)
            y = jnp.zeros((T, d), x_flat.dtype).at[tok].add(w[:, None] * gathered)
            return y

        def _shared_mlp(x_flat, shared_w_up_gate, shared_w_down):
            gu = jnp.einsum('td,dm->tm', x_flat, shared_w_up_gate)
            gate, up = jnp.split(gu, [J], axis=-1)
            return jnp.einsum('tm,md->td', jax.nn.silu(gate) * up, shared_w_down)
        b, s, d = x.shape
        x_flat = x.reshape(b * s, d)
        routed = _moe_routed(x_flat, router, w_up_gate, w_down)
        shared = _shared_mlp(x_flat, shared_w_up_gate, shared_w_down)
        return (routed + shared).reshape(b, s, d)
    x = x + jnp.tanh(g_xattn[0]) * _L0_xattn_ref(_layernorm(x, axis=-1), ctx_512, L0_xattn_Wq, L0_xattn_w_kc_q, L0_xattn_w_kc_kv, L0_xattn_W_qr, L0_xattn_W_kr, L0_xattn_Wo)
    x = x + jnp.tanh(g_ffn[0]) * _L0_ffn_ref(_layernorm(x, axis=-1), L0_ffn_router, L0_ffn_w_up_gate, L0_ffn_w_down, L0_ffn_shared_w_up_gate, L0_ffn_shared_w_down)
    return x

_drawn_inputs = setup_inputs


def setup_inputs(seed=0):
    import zlib

    import numpy as np

    out = dict(_drawn_inputs(seed))
    spreads = {}
    factors = {'L0_ffn_router': 4.12, 'L0_ffn_w_up_gate': 3.584, 'L0_ffn_w_down': 3.594}
    for name, (base, spread) in spreads.items():
        noise = np.random.default_rng([zlib.crc32(name.encode()), seed]).standard_normal(out[name].shape)
        drawn = base * np.exp(spread * noise) if base else spread * noise
        out[name] = jnp.asarray(drawn.astype(out[name].dtype))
    for name, factor in factors.items():
        out[name] = (out[name] * factor).astype(out[name].dtype)
    return out
```

```python
from contextlib import ExitStack

import concourse.bass as bass
from concourse import mybir

F32 = mybir.dt.float32
BF16 = mybir.dt.bfloat16
I32 = mybir.dt.int32
ALU = mybir.AluOpType
ACT = mybir.ActivationFunctionType
AX = mybir.AxisListType

P = 128
NB = 32
S = 128
D = 512
KT = D // P
H = 16
R = 64
DQ = 384
NPAIR = H // 2
UPB = 4
NU = NB * UPB
NG = NB // 2
EPS = 1e-5
RSQRT_SEED = float(0x5F3759DF)
RSQRT_OPS = 17

E = 8
I = 352
CAP = 1280
J = 1408
JT = J // P
SLICE = KT * 2 * P + D
PIECE = SLICE // 2
IT = 3
IW = [P, P, I - 2 * P]
XW = KT * 2 * I + IT * D
XPIECE = XW // 4
TPX = CAP // P
NQ = E * TPX // 2

HI, LO = 0, 1
PASSES = ((HI, HI), (HI, LO), (LO, HI))

FIRST_STEP, LOOP_STEP, LOOPS, LAST_STEP = -24, 16, 5, 135
FFN_FIRST = 98
BODY = 16


def build(nc, x, kv_t, kv_n, gates, Wq, w_qk, W_qr, W_kr, w_kv, Wo_t, router, tables, ident, w_shared, w_expert,
          route_const, token_ids, out):
    ctx = ExitStack()
    with ctx:
        def sem(name):
            return ctx.enter_context(nc.semaphore(name))

        def bank(name):
            return ctx.enter_context(nc.psum_tensor(name, [P, 512], F32))

        ARENA = 52900
        arena = ctx.enter_context(nc.sbuf_tensor("arena", [P, ARENA], F32))
        taken = [0]

        def words(n):
            at = taken[0]
            taken[0] += n
            assert taken[0] <= ARENA, taken[0]
            return arena[:, at:at + n]

        def halves(region):
            return region.bitcast(BF16)

        ident_sb = words(P)
        table_sb = words(4 * P)
        router_sb = words(KT * E)
        gate_sb = words(2)
        tanh_sb = words(2)
        route_sb = words(2 * P + E)
        token_sb = words(NB).bitcast(I32)
        one, waited = words(1), words(16)
        zero_ids = words(E * CAP // P).bitcast(I32)
        logits = words(NB * E).rearrange("p (b e) -> p b e", e=E)
        slot_of = words(2 * NB).bitcast(I32).rearrange("p (b c) -> p b c", c=2)
        scatter_to = words(2 * NB).bitcast(I32).rearrange("p (b c) -> p b c", c=2)
        weight_of = words(2 * NB).rearrange("p (b c) -> p b c", c=2)

        bm_at = taken[0]
        B_region = words(2 * KT * H * R // 2)
        B_w = halves(B_region).rearrange("p (l t n) -> p l t n", l=2, t=KT)
        M_region = words(2 * H * D // 2)
        M_w = halves(M_region).rearrange("p (l h n) -> p l h n", l=2, h=H)
        BM_region = arena[:, bm_at:taken[0]]
        k_region = words(2 * NPAIR * 512)
        work_at = taken[0]
        Kr_w = halves(words(H * R)).rearrange("p (l n) -> p l n", l=2)
        q_region = words(2 * NPAIR * 256)
        qT = [halves(q_region[:, g * 2048:(g + 1) * 2048]).rearrange("p (l m n) -> p l m n", l=2, m=NPAIR)
              for g in range(2)]
        kblk = [halves(k_region[:, g * 4096:(g + 1) * 4096]).rearrange("p (l m b n) -> p l m b n", l=2, m=NPAIR, b=2)
                for g in range(2)]
        xT1_region = words(2 * KT * 256)
        xT1 = [halves(xT1_region[:, g * 1024:(g + 1) * 1024]).rearrange("p (l t n) -> p l t n", l=2, t=KT)
               for g in range(2)]
        kvT_region = words(2 * 256)
        kvT = [halves(kvT_region[:, g * 256:(g + 1) * 256]).rearrange("p (l n) -> p l n", l=2) for g in range(2)]
        kvN_region = words(2 * 256)
        kvN = [halves(kvN_region[:, g * 256:(g + 1) * 256]).rearrange("p (l b n) -> p l b n", l=2, b=2)
               for g in range(2)]
        kvT_raw = words(512).rearrange("p (r n) -> p r n", r=2)
        kvN_raw = words(256).rearrange("p (b n) -> p b n", b=2)
        rope_a = words(256)
        rope_b = words(256)
        prob_region = words(4 * 512)
        prob = prob_region.rearrange("p (u h n) -> p u h n", u=4, h=4)
        kr_at = taken[0]
        pT_region = words(512)
        pT = halves(pT_region).rearrange("p (l n) -> p l n", l=2)
        cT_region = words(512)
        cT = halves(cT_region).rearrange("p (l h n) -> p l h n", l=2, h=4)
        neg_max = words(16).rearrange("p (u h) -> p u h", u=4)
        den = words(16).rearrange("p (u h) -> p u h", u=4)
        rden = words(16).rearrange("p (u h) -> p u h", u=4)
        x_ln = words(2 * D).rearrange("p (b n) -> p b n", b=2)
        xn1 = words(2 * D).rearrange("p (b n) -> p b n", b=2)
        x1 = words(2 * D).rearrange("p (b n) -> p b n", b=2)
        xn2 = words(2 * D).rearrange("p (b n) -> p b n", b=2)
        xT32 = words(2 * D).rearrange("p (b n) -> p b n", b=2)
        xT2 = [halves(words(D)).rearrange("p (l t n) -> p l t n", l=2, t=KT) for _ in range(2)]
        stats = words(4 * 6).rearrange("p (c n) -> p c n", c=4)
        mean = words(4)
        mean_dif = words(4)
        var_eps = words(4)
        shifted = words(4)
        rstd = words(4)
        newton = words(4)
        work_region = arena[:, work_at:taken[0]]
        stage = words(2 * H * (D // 2 + 32))
        wqk_sb = stage[:, 0:3 * H * P].rearrange("p (t h k) -> p t h k", t=3, h=H)
        wqr_sb = stage[:, 3 * H * P:3 * H * (P + R)].rearrange("p (t h r) -> p t h r", t=3, h=H)
        Wq_sb = M_region.rearrange("p (h d) -> p h d", h=H)
        A_sb = prob_region[:, 0:H * R].rearrange("p (h r) -> p h r", h=H)
        assert pT_region.shape == cT_region.shape
        kr_stage = arena[:, kr_at:kr_at + H * R]
        wo_wkv = words(4 * (D + P))
        wo_ring = wo_wkv[:, 0:4 * D].rearrange("p (s n) -> p s n", s=4)
        wkv_ring = wo_wkv[:, 4 * D:].rearrange("p (s n) -> p s n", s=4)


        wsh_raw = wo_wkv[:, 0:3 * PIECE].rearrange("p (s n) -> p s n", s=3)
        wsh = [halves(stage[:, i * SLICE:(i + 1) * SLICE]).rearrange("p (l n) -> p l n", l=2) for i in range(6)]
        wsh += [halves(k_region[:, i * SLICE:(i + 1) * SLICE]).rearrange("p (l n) -> p l n", l=2) for i in range(5)]
        wx = [halves(BM_region[:, i * XW:(i + 1) * XW]).rearrange("p (l n) -> p l n", l=2) for i in range(2)]
        spare = [BM_region[:, 2 * XW:], work_region]
        used = [0, 0]

        def reuse(n, r=1):
            at = used[r]
            used[r] += n
            assert used[r] <= spare[r].shape[1], (used, spare[r].shape)
            return spare[r][:, at:at + n]

        wx_raw = reuse(2 * XPIECE, 0).rearrange("p (s n) -> p s n", s=2)
        xs = [halves(reuse(4 * D)).rearrange("p (b n) -> p b n", b=4) for _ in range(2)]
        hsh = [halves(reuse(512)).rearrange("p (l n) -> p l n", l=2) for _ in range(2)]
        silu = [reuse(512) for _ in range(2)]
        h32 = [reuse(512) for _ in range(2)]
        y_sb = reuse(4 * D).rearrange("p (b n) -> p b n", b=4)
        either = reuse(8 * D)
        r_sb = either.rearrange("p (r n) -> p r n", r=8)
        xg = [either[:, i * 1024:(i + 1) * 1024].rearrange("p (b n) -> p b n", b=2) for i in range(2)]
        xgT = [halves(either[:, 2048 + i * 1024:3072 + i * 1024]).rearrange("p (l t n) -> p l t n", l=2, t=KT)
               for i in range(2)]
        hx = [halves(reuse(IT * 256)).rearrange("p (l j n) -> p l j n", l=2, j=IT) for _ in range(2)]
        xo = reuse(4 * D).rearrange("p (s n) -> p s n", s=4)
        ids = reuse(2 * TPX).bitcast(I32).rearrange("p (s n) -> p s n", s=2)
        slot_now = reuse(8).bitcast(I32)
        weight_now = reuse(8)
        N8 = NB * E
        mask32, rt_a, rt_b, rt_rank, rt_count = (either[:, i * N8:(i + 1) * N8] for i in range(5))
        rt_hot = either[:, 5 * N8:7 * N8].rearrange("p (c n) -> p c n", c=2)
        rt_sum = either[:, 7 * N8:7 * N8 + 2 * (P + N8)].rearrange("p (c n) -> p c n", c=2)
        small = either[:, 10 * N8:10 * N8 + 10 * NB]
        rt_top, rt_rev, rt_share = (small[:, 2 * i * NB:2 * (i + 1) * NB].rearrange("p (c n) -> p c n", c=2)
                                    for i in range(3))
        rt_gap, rt_exp, rt_pos, rt_valid = (small[:, (6 + i) * NB:(7 + i) * NB] for i in range(4))
        rt_c = either[:, 11 * N8 + 2 * NB:11 * N8 + 3 * NB]

        score_bank = [bank("score0"), bank("score1")]
        t_bank = bank("t_bank")
        c_bank = bank("c_bank")
        o_bank = [bank("o0"), bank("o1")]
        p_bank = bank("p_bank")
        m_bank = bank("m_bank")
        ab_bank = [score_bank[0], score_bank[1], o_bank[0], o_bank[1]]
        acc_bank = [o_bank[0], o_bank[1], t_bank, c_bank]
        gate_bank = [score_bank[0], p_bank]
        up_bank = [score_bank[1], m_bank]
        xt_bank = [t_bank, c_bank]
        gu_bank = [score_bank[0], score_bank[1]]
        xd_bank = [o_bank[0], o_bank[1]]

        x1_d = nc.dram_tensor("x1_d", [NB, S, D], F32, kind="Internal").ap()
        xn2_d = nc.dram_tensor("xn2_d", [NB, S, D], F32, kind="Internal").ap()
        xT2_d = nc.dram_tensor("xT2_d", [NB, P, 2 * D], BF16, kind="Internal").ap()
        y_d = nc.dram_tensor("y_d", [8, S, D], F32, kind="Internal").ap()
        slot_token_d = nc.dram_tensor("slot_token_d", [E * CAP, 1], I32, kind="Internal").ap()
        xrow_d = nc.dram_tensor("xrow_d", [E * CAP, D], F32, kind="Internal").ap()

        const_in = sem("const_in")
        wqk_in, wqr_in, wq_in, kr_in = sem("wqk_in"), sem("wqr_in"), sem("wq_in"), sem("kr_in")
        wo_in = [sem(f"wo_in{i}") for i in range(4)]
        a_mm, a_copied, b_mm, b_hi, b_lo = sem("a_mm"), sem("a_copied"), sem("b_mm"), sem("b_hi"), sem("b_lo")
        kr_hi, kr_lo = sem("kr_hi"), sem("kr_lo")
        m_mm, m_hi, m_lo = sem("m_mm"), sem("m_hi"), sem("m_lo")
        tanh_done, kblk_zero = sem("tanh_done"), sem("kblk_zero")
        xln_in, kvt_in, kvn_in = sem("xln_in"), sem("kvt_in"), sem("kvn_in")
        xres_in = [sem("xres_in0"), sem("xres_in1")]
        x1_out = [sem("x1_out0"), sem("x1_out1")]
        xn2_out = [sem("xn2_out0"), sem("xn2_out1")]
        xT2_out = [sem("xT2_out0"), sem("xT2_out1")]
        scored, maxed, exped, inverted, normed = (sem("scored"), sem("maxed"), sem("exped"), sem("inverted"),
                                                  sem("normed"))
        pt_mm, pt_hi, pt_lo = sem("pt_mm"), sem("pt_hi"), sem("pt_lo")
        ct_mm, ct_hi, ct_lo = sem("ct_mm"), sem("ct_hi"), sem("ct_lo")
        o_mm, x1_done = sem("o_mm"), sem("x1_done")
        pr_mm, pr_hi, pr_lo = sem("pr_mm"), sem("pr_hi"), sem("pr_lo")
        ln_mm = {"l1": sem("l1_mm"), "l2": sem("l2_mm")}
        ln_up = {"l1": sem("l1_up"), "l2": sem("l2_up")}
        ln_lo = {"l1": sem("l1_lo"), "l2": sem("l2_lo")}
        lg_mm, lg_up = sem("lg_mm"), sem("lg_up")
        stat1, stat2 = sem("stat1"), sem("stat2")
        rsqrt_step, xn1_ready, xn2_ready = sem("rsqrt_step"), sem("xn1_ready"), sem("xn2_ready")
        ropeT_step, ropeN_step = sem("ropeT_step"), sem("ropeN_step")

        wsh_in = [sem(f"wsh_in{i}") for i in range(3)]
        wsh_hi, wsh_lo = sem("wsh_hi"), sem("wsh_lo")
        xs_in = [sem("xs_in0"), sem("xs_in1")]
        y_in, y_out = sem("y_in"), sem("y_out")
        gu_mm, silu_done, h_mul, h_hi, h_lo = sem("gu_mm"), sem("silu_done"), sem("h_mul"), sem("h_hi"), sem("h_lo")
        acc_mm, y_done, comb_1, comb_2 = sem("acc_mm"), sem("y_done"), sem("comb_1"), sem("comb_2")
        route_step, masked, ranked, rank_up = sem("route_step"), sem("masked"), sem("ranked"), sem("rank_up")
        gap_done, exp_done, routed = sem("gap_done"), sem("exp_done"), sem("routed")
        zeroed, ids_zero, scattered = sem("zeroed"), sem("ids_zero"), sem("scattered")
        ids_in = [sem("ids_in0"), sem("ids_in1")]
        wx_in = [sem("wx_in0"), sem("wx_in1")]
        wx_hi, wx_lo = sem("wx_hi"), sem("wx_lo")
        xg_in = [sem("xg_in0"), sem("xg_in1")]
        xt_mm, xt_hi, xt_lo = sem("xt_mm"), sem("xt_hi"), sem("xt_lo")
        xgu_mm, xsilu, xmul, xhh, xhl = sem("xgu_mm"), sem("xsilu"), sem("xmul"), sem("xhh"), sem("xhl")
        xd_mm, xo_up = sem("xd_mm"), sem("xo_up")
        xo_out = [sem(f"xo_out{i}") for i in range(4)]
        now_done, r_in = sem("now_done"), sem("r_in")

        block = ctx.enter_context(nc.Block())

        def wait(eng, s, c, per, it):
            if it is None:
                if c > 0:
                    eng.wait_ge(s, c)
            else:
                assert c > 0
                eng.wait_ge(s, it * per + c)

        def at(c, per, it):
            return c if it is None else it * per + c

        def run_steps(eng, step):
            for k in range(-12, LOOP_STEP):
                step(k, None)
            with eng.Fori(0, LOOPS) as it:
                for k in range(LOOP_STEP, LOOP_STEP + BODY):
                    step(k, it)
            for k in range(LOOP_STEP + BODY * LOOPS, LAST_STEP + 1):
                step(k, None)

        def within(i, n):
            return 0 <= i < n

        def run_shared(eng, step):
            for v in range(22, 33):
                step(v, None)
            with eng.Fori(0, 2) as it:
                for v in range(33, 55):
                    step(v, it)
            for v in range(77, 89):
                step(v, None)

        def run_experts(eng, step):
            for k in range(-1, 3):
                step(k, None)
            with eng.Fori(0, 3) as it:
                for k in range(3, 13):
                    step(k, it)
            for k in range(33, NQ + 1):
                step(k, None)

        def attention_over(eng):
            for s, c in ((o_mm, NB), (x1_done, NB), (lg_mm, NB), (lg_up, NB), (xn2_ready, NB), (ln_lo["l2"], NB),
                         (ropeN_step, 6 * NG)):
                eng.wait_ge(s, c)
            for p in range(2):
                for s in (x1_out, xn2_out, xT2_out):
                    eng.wait_ge(s[p], 16 * NB // 2)

        @block.sync
        def _(sp):
            def step(k, it):
                m = k % 8
                if m == 1:
                    g = (k + 23) // 8
                    if within(g, NG):
                        wait(sp, ropeT_step, 5 * g, 10, it)
                        sp.dma_start(kvT_raw, kv_t[at(g, 2, it)]).then_inc(kvt_in, 16)
                if m == 5:
                    g = (k + 11) // 8
                    if within(g, NG):
                        wait(sp, ropeN_step, 6 * g, 12, it)
                        sp.dma_start(kvN_raw, kv_n[at(g, 2, it)]).then_inc(kvn_in, 16)
                if k % 4 == 0 and within(k // 4 - 1, NB):
                    b = k // 4 - 1
                    wait(sp, x1_done, b + 1, 4, it)
                    sp.dma_start(x1_d[at(b, 4, it)], x1[:, b % 2, :]).then_inc(x1_out[b % 2], 16)
                if m == 2:
                    g = (k + 22) // 8
                    if within(g, NG):
                        wait(sp, xn1_ready, 2 * g, 4, it)
                        sp.dma_start(x_ln, x_g[at(g, 2, it)]).then_inc(xln_in, 16)
                    g = k // 8 - 1
                    for b in (2 * g, 2 * g + 1):
                        if within(b, NB):
                            wait(sp, xn2_ready, b + 1, 4, it)
                            sp.dma_start(xn2_d[at(b, 4, it)], xn2[:, b % 2, :]).then_inc(xn2_out[b % 2], 16)
                    for b in (2 * g + 2, 2 * g + 3):
                        if within(b, NB):
                            wait(sp, x1_out[b % 2], 16 * (b // 2), 32, it)
                            wait(sp, xn2_ready, b - 1, 4, it)
                            sp.dma_start(x1[:, b % 2, :], x[at(b, 4, it)]).then_inc(xres_in[b % 2], 16)
                if m in (6, 7):
                    b = 2 * (k // 8 - 1) + m - 6
                    if within(b, NB):
                        wait(sp, ln_lo["l2"], b + 1, 4, it)
                        sp.dma_start(xT2_d[at(b, 4, it)],
                                     xT2[b % 2].rearrange("p l t n -> p (l t n)")).then_inc(xT2_out[b % 2], 16)
                if -8 <= k < 0:
                    for h in (2 * (k + 8), 2 * (k + 8) + 1):
                        load_m(h)
                if it is None and within(k - FFN_FIRST + 1, 12):
                    load_wsh(k - FFN_FIRST + 1)

            x_g = x.rearrange("(g b) s d -> g s b d", b=2)
            wo_h = Wo_t.rearrange("(h k) n -> h k n", h=H)

            def load_m(h):
                wait(sp, m_mm, h - 3, 0, None)
                sp.dma_start(wo_ring[:, h % 4, :], wo_h[h]).then_inc(wo_in[h % 4], 16)
                sp.dma_start(wkv_ring[:, h % 4, :], w_kv[h]).then_inc(wo_in[h % 4], 16)

            def load_wsh(n):
                sp.wait_ge(m_mm, H)
                wait(sp, wsh_lo, n - 2, 0, None)
                sp.dma_start(wsh_raw[:, n % 3, :], w_shared[n // 2, :, (n % 2) * PIECE:(n % 2 + 1) * PIECE])\
                    .then_inc(wsh_in[n % 3], 16)

            def load_wx(n, it):
                wait(sp, wx_lo, n - 1, 8, it)
                sp.dma_start(wx_raw[:, n % 2, :], w_x[at(n // 4, 2, it), n % 4]).then_inc(wx_in[n % 2], 16)

            w_x = w_expert.rearrange("e p (r n) -> e r p n", r=4)
            step(-22, None)
            step(-23, None)
            sp.dma_start(route_sb, route_const).then_inc(const_in, 16)
            sp.dma_start(token_sb, token_ids).then_inc(const_in, 16)
            sp.dma_start(ident_sb, ident).then_inc(const_in, 16)
            sp.dma_start(table_sb, tables).then_inc(const_in, 16)
            sp.dma_start(gate_sb, gates).then_inc(const_in, 16)
            sp.dma_start(router_sb.rearrange("p (t e) -> p t e", t=KT),
                         router.rearrange("(t p) e -> p t e", t=KT)).then_inc(const_in, 16)
            sp.dma_start(wqk_sb.rearrange("p t h k -> p t (h k)"),
                         w_qk.rearrange("(t p) n -> p t n", t=3)).then_inc(wqk_in, 16)
            sp.dma_start(wqr_sb.rearrange("p t h r -> p t (h r)"),
                         W_qr.rearrange("(t p) n -> p t n", t=3)).then_inc(wqr_in, 16)
            sp.dma_start(Wq_sb, Wq.rearrange("(h k) d -> k h d", h=H)).then_inc(wq_in, 16)
            sp.dma_start(kr_stage, W_kr).then_inc(kr_in, 16)
            for k in range(-21, -12):
                step(k, None)
            sp.wait_ge(zeroed, 2)
            sp.dma_start(slot_token_d.rearrange("(p c) o -> p (c o)", p=P), zero_ids).then_inc(ids_zero, 16)
            run_steps(sp, step)

            xT2_g = xT2_d.rearrange("(g b) p n -> g p b n", b=4)
            x1_t = x1_d.rearrange("(g b) s d -> g s b d", b=4)
            y_t = y_d.rearrange("(g b) s d -> g s b d", b=4)
            attention_over(sp)
            for g in range(2):
                sp.dma_start(xs[g], xT2_g[g]).then_inc(xs_in[g], 16)
            sp.dma_start(y_sb, x1_t[0]).then_inc(y_in, 16)
            for n in range(12, 2 * JT):
                load_wsh(n)
            for t in range(4):
                sp.wait_ge(y_done, t + 1)
                sp.dma_start(y_d[t], y_sb[:, t, :]).then_inc(y_out, 16)
            sp.wait_ge(y_out, 64)
            sp.dma_start(y_sb, x1_t[1]).then_inc(y_in, 16)
            for r in range(4):
                load_wx(r, None)

            def load_ids(e, it):
                wait(sp, xt_mm, 5 * (e - 1), 10, it)
                sp.dma_start(ids[:, e % 2, :], ids_e[at(e, 2, it)]).then_inc(ids_in[e % 2], 16)

            ids_e = slot_token_d.rearrange("(e p c) o -> e p (c o)", e=E, p=P)
            sp.wait_ge(scattered, 64 * 16)
            load_ids(0, None)
            for t in range(4):
                sp.wait_ge(y_done, 4 + t + 1)
                sp.dma_start(y_d[4 + t], y_sb[:, t, :]).then_inc(y_out, 16)

            xrow_v = xrow_d.rearrange("(e p c) d -> e c p d", e=E, p=P)

            def expert_step(k, it):
                e = (k + 5) // 5
                if e >= 1 and e < E and k % 5 == 0:
                    load_ids(e, it)
                if 1 <= e < E and k % 5 < 4:
                    load_wx(4 * e + k % 5, it)
                q = k - 1
                if within(q, NQ):
                    for t in range(2):
                        n = 2 * q + t
                        wait(sp, xo_up, n + 1, 20, it)
                        sp.dma_start(xrow_v[at(q // 5, 2, it), 2 * (q % 5) + t], xo[:, n % 4, :])\
                            .then_inc(xo_out[n % 4], 16)

            for g in (2, 3):
                sp.dma_start(xs[g % 2], xT2_g[g]).then_inc(xs_in[g % 2], 16)
            sp.wait_ge(y_out, 16 * 8)
            sp.dma_start(y_sb, y_t[0]).then_inc(y_in, 16)
            run_experts(sp, expert_step)

            def shared_step(v, it):
                g, m = v // JT, v % JT
                if v in (28, 32):
                    sp.wait_ge(y_out, 16 * (12 if v == 28 else 16))
                    sp.dma_start(y_sb, y_t[1] if v == 28 else x1_t[2]).then_inc(y_in, 16)
                if 24 <= v < 32:
                    t = v - 24
                    store_out(t, t, None)
                if v >= 34 and 1 <= m <= 4:
                    t = 4 * (g - 1) + m - 1
                    store_out(t, t, it)
                if v >= 34 and m == 5 and g < 8:
                    wait(sp, y_out, 16 * 4 * (g + 2), 128, it)
                    sp.dma_start(y_sb, x1_t[at(g, 2, it)]).then_inc(y_in, 16)
                if m == 0 and 3 <= g < 7:
                    wait(sp, gu_mm, 11 * g, 22, it)
                    sp.dma_start(xs[(g + 1) % 2], xT2_g[at(g + 1, 2, it)]).then_inc(xs_in[(g + 1) % 2], 16)

            def store_out(t, c, it):
                wait(sp, comb_2, c + 1, 8, it)
                sp.dma_start(out[at(t, 8, it)], y_sb[:, t % 4, :]).then_inc(y_out, 16)

            run_shared(sp, shared_step)
            for t in range(28, 32):
                store_out(t, t, None)
            sp.wait_ge(y_out, 16 * 40)

        @block.tensor
        def _(pe):
            def step(k, it):
                m = k % 8
                u = k
                if within(u, NU):
                    b, hg = u // 4, u % 4
                    wait(pe, ct_lo, u + 1, 16, it)
                    if hg == 0:
                        wait(pe, x1_done, b - 1, 4, it)
                        if u == 0:
                            pe.wait_ge(m_lo, H)
                    n = 0
                    for h in range(4):
                        for a, w in PASSES:
                            mm = pe.matmul(o_bank[b % 2][:, :], lhsT=cT[:, a, h, :], rhs=M_w[:, w, 4 * hg + h, :],
                                           start=(hg == 0 and n == 0), stop=(hg == 3 and n == 11))
                            n += 1
                    if hg == 3:
                        mm.then_inc(o_mm, 1)
                u = k + 1
                if within(u, NU):
                    g, b = u // 8, u // 4
                    wait(pe, pt_lo, u + 1, 16, it)
                    wait(pe, ct_lo, u, 16, it)
                    if u % 8 == 0:
                        wait(pe, ropeN_step, 6 * (g + 1), 12, it)
                    for n, (a, w) in enumerate(PASSES):
                        mm = pe.matmul(c_bank[:, :], lhsT=kvN[g % 2][:, a, b % 2, :], rhs=pT[:, w, :],
                                       start=(n == 0), stop=(n == 2))
                    mm.then_inc(ct_mm, 1)
                u = k + 2
                if within(u, NU):
                    wait(pe, normed, u + 1, 16, it)
                    wait(pe, pt_lo, u, 16, it)
                    for h in range(4):
                        mm = pe.transpose(t_bank[:, h * S:(h + 1) * S], prob[:, u % 4, h, :], ident_sb)
                    mm.then_inc(pt_mm, 1)
                u = k + 4
                if within(u, NU):
                    g, b, hg = u // 8, u // 4, u % 4
                    wait(pe, exped, u - 1, 16, it)
                    wait(pe, pr_lo, 8 * g + 2 * hg + 2, 16, it)
                    for pr in range(2):
                        mp = 2 * hg + pr
                        for n, (a, w) in enumerate(PASSES):
                            mm = pe.matmul(score_bank[u % 2][:, pr * 256:(pr + 1) * 256],
                                           lhsT=qT[g % 2][:, a, mp, (b % 2) * S:(b % 2 + 1) * S],
                                           rhs=kblk[g % 2][:, w, mp, b % 2, :], start=(n == 0), stop=(n == 2))
                    mm.then_inc(scored, 1)
                q = k + 12
                if within(q, 8 * NG):
                    g, j = q // 8, q % 8
                    wait(pe, pr_lo, q, 16, it)
                    if j == 0:
                        wait(pe, ln_lo["l1"], 2 * (g + 1), 4, it)
                    if j == 1:
                        wait(pe, ropeT_step, 5 * (g + 1), 10, it)
                    for half in range(2):
                        mp = 2 * (j // 2) + half
                        cols = slice(mp * P, (mp + 1) * P)
                        o = p_bank[:, half * 256:(half + 1) * 256]
                        if j % 2 == 0:
                            for n in range(3 * KT):
                                t, (a, w) = n // 3, PASSES[n % 3]
                                mm = pe.matmul(o, lhsT=B_w[:, a, t, cols], rhs=xT1[g % 2][:, w, t, :],
                                               start=(n == 0), stop=(n == 3 * KT - 1))
                        else:
                            for n, (a, w) in enumerate(PASSES):
                                mm = pe.matmul(o, lhsT=Kr_w[:, a, cols], rhs=kvT[g % 2][:, w, :],
                                               start=(n == 0), stop=(n == 2))
                    mm.then_inc(pr_mm, 1)
                if -8 <= k < 0:
                    fuse_m(2 * (k + 8))
                    fuse_m(2 * (k + 8) + 1)
                misc(k, it)

            def misc_free(t1, b, bl, it):
                for s, c, top in ((ln_up["l1"], t1, NB), (ln_up["l2"], b, NB), (lg_up, bl, NB)):
                    wait(pe, s, min(c, top) if it is None else c, 4, it)

            def misc(k, it):
                m = k % 8
                c = k // 8
                if m in (2, 3):
                    t1 = 2 * (c + 2) + m - 2
                    if within(t1, NB):
                        wait(pe, xn1_ready, t1 + 1, 4, it)
                        misc_free(t1, 2 * (c - 1), 2 * (c - 1), it)
                        ln_transposes(xn1[:, t1 % 2, :], ln_mm["l1"])
                if m in (4, 5):
                    b = 2 * (c - 1) + m - 4
                    if within(b, NB):
                        wait(pe, xn2_ready, b + 1, 4, it)
                        misc_free(2 * (c + 3), b, 2 * (c - 1), it)
                        ln_transposes(xn2[:, b % 2, :], ln_mm["l2"])
                if m in (6, 7):
                    b = 2 * (c - 1) + m - 6
                    if within(b, NB):
                        wait(pe, ln_up["l2"], b + 1, 4, it)
                        misc_free(2 * (c + 3), 2 * c, b, it)
                        for t in range(KT):
                            mm = pe.matmul(m_bank[:, 0:E], lhsT=xT32[:, b % 2, t * P:(t + 1) * P],
                                           rhs=router_sb[:, t * E:(t + 1) * E], start=(t == 0), stop=(t == KT - 1))
                        mm.then_inc(lg_mm, 1)

            def ln_transposes(rows, done):
                for t in range(KT):
                    mm = pe.transpose(m_bank[:, t * P:(t + 1) * P], rows[:, t * P:(t + 1) * P], ident_sb)
                mm.then_inc(done, 1)

            def fuse_m(h):
                pe.wait_ge(wo_in[h % 4], 32 * (h // 4 + 1))
                if h < 2:
                    pe.wait_ge(b_lo, 8)
                else:
                    pe.wait_ge(m_lo, h - 1)
                pe.matmul(o_bank[h % 2][:, :], lhsT=wkv_ring[:, h % 4, :], rhs=wo_ring[:, h % 4, :],
                          start=True, stop=True).then_inc(m_mm, 1)

            pe.wait_ge(const_in, 96)
            pe.wait_ge(wqk_in, 16)
            pe.wait_ge(wqr_in, 16)
            for half in range(2):
                for h in range(8):
                    for t in range(3):
                        mm = pe.matmul(ab_bank[half][:, h * R:(h + 1) * R], lhsT=wqk_sb[:, t, 8 * half + h, :],
                                       rhs=wqr_sb[:, t, 8 * half + h, :], start=(t == 0), stop=(t == 2))
                mm.then_inc(a_mm, 1)
            pe.wait_ge(wq_in, 16)
            pe.wait_ge(a_copied, 2)
            for n in range(8):
                half, t = n // KT, n % KT
                if n >= 4:
                    pe.wait_ge(b_lo, n - 3)
                for h in range(8):
                    mm = pe.matmul(ab_bank[(n + 2) % 4][:, h * R:(h + 1) * R],
                                   lhsT=Wq_sb[:, 8 * half + h, t * P:(t + 1) * P], rhs=A_sb[:, 8 * half + h, :],
                                   start=True, stop=True)
                mm.then_inc(b_mm, 1)
            for k in range(FIRST_STEP, -12):
                step(k, None)
            pe.wait_ge(b_lo, 8)
            pe.wait_ge(kr_lo, 1)
            run_steps(pe, step)

            def gate_up(v, it):
                g, m = v // JT, v % JT
                wait(pe, h_mul, v - 1, 22, it)
                if m == 0:
                    wait(pe, xs_in[g % 2], 16 * (g // 2 + 1), 16, it)
                if g == 0:
                    pe.wait_ge(wsh_lo, 2 * (m + 1))
                for c, dst in enumerate((gate_bank[v % 2], up_bank[v % 2])):
                    for n in range(3 * KT):
                        t, (a, w) = n // 3, PASSES[n % 3]
                        col = t * 2 * P + c * P
                        mm = pe.matmul(dst[:, :].rearrange("p (b n) -> p b n", b=4), lhsT=wsh[m][:, a, col:col + P],
                                       rhs=xs[g % 2][:, :, w * D + t * P:w * D + (t + 1) * P],
                                       start=(n == 0), stop=(n == 3 * KT - 1))
                mm.then_inc(gu_mm, 1)

            def down(v, it):
                g, m = v // JT, v % JT
                wait(pe, h_lo, v + 1, 22, it)
                if m == 0:
                    wait(pe, y_done, 4 * g, 8, it)
                for t in range(4):
                    for n, (a, w) in enumerate(PASSES):
                        mm = pe.matmul(acc_bank[t][:, :], lhsT=hsh[v % 2][:, a, t * P:(t + 1) * P],
                                       rhs=wsh[m][:, w, KT * 2 * P:], start=(m == 0 and n == 0),
                                       stop=(m == JT - 1 and n == 2))
                if m == JT - 1:
                    mm.then_inc(acc_mm, 1)

            pe.wait_ge(x1_done, NB)
            pe.wait_ge(lg_up, NB)
            for v in range(22):
                if v == 4:
                    pe.wait_ge(masked, 1)
                    pe.wait_ge(h_mul, 3)
                    pe.matmul(gate_bank[0][:, 0:N8], lhsT=route_sb[:, 0:P], rhs=mask32, start=True, stop=True)
                    pe.matmul(gate_bank[0][:, N8:2 * N8], lhsT=route_sb[:, P:2 * P], rhs=mask32,
                              start=True, stop=True).then_inc(ranked, 1)
                    down(3, None)
                    pe.wait_ge(rank_up, 1)
                gate_up(v, None)
                if v not in (0, 4):
                    down(v - 1, None)
            down(21, None)
            pe.wait_ge(y_done, 8)

            def expert_step(k, it):
                if within(k, NQ):
                    expert_gate_up(k, 0, it)
                if within(k + 1, NQ):
                    q = k + 1
                    wait(pe, xg_in[q % 2], 32 * (q // 2 + 1), 160, it)
                    wait(pe, xt_lo, 2 * q, 20, it)
                    for t in range(KT):
                        for b in range(2):
                            mm = pe.transpose(xt_bank[t // 2][:, (t % 2) * 256 + b * P:(t % 2) * 256 + (b + 1) * P],
                                              xg[q % 2][:, b, t * P:(t + 1) * P], ident_sb)
                    mm.then_inc(xt_mm, 1)
                if within(k, NQ):
                    expert_gate_up(k, 1, it)
                if within(k - 1, NQ):
                    expert_down(k - 1, 0, it)
                if within(k, NQ):
                    expert_gate_up(k, 2, it)
                if within(k - 1, NQ):
                    expert_down(k - 1, 1, it)

            def expert_gate_up(q, j, it):
                e = q // 5
                if j == 0:
                    wait(pe, xt_lo, 2 * (q + 1), 20, it)
                    if q % 5 == 0:
                        wait(pe, wx_lo, 4 * (e + 1), 8, it)
                n1 = 3 * q + j
                wait(pe, xmul, n1 - 1, 30, it)
                for c in range(2):
                    for n in range(3 * KT):
                        t, (a, w) = n // 3, PASSES[n % 3]
                        col = t * 2 * I + c * I + j * P
                        mm = pe.matmul(gu_bank[n1 % 2][0:IW[j], c * 256:(c + 1) * 256],
                                       lhsT=wx[e % 2][:, a, col:col + IW[j]], rhs=xgT[q % 2][:, w, t, :],
                                       start=(n == 0), stop=(n == 3 * KT - 1))
                mm.then_inc(xgu_mm, 1)

            def expert_down(q, b, it):
                e = q // 5
                n1 = 2 * q + b
                if b == 0:
                    wait(pe, xhl, 3 * (q + 1), 30, it)
                wait(pe, xo_up, n1 - 1, 20, it)
                for j in range(IT):
                    for n, (a, w) in enumerate(PASSES):
                        col = KT * 2 * I + j * D
                        mm = pe.matmul(xd_bank[b][:, :], lhsT=hx[q % 2][0:IW[j], a, j, b * P:(b + 1) * P],
                                       rhs=wx[e % 2][0:IW[j], w, col:col + D], start=(j == 0 and n == 0),
                                       stop=(j == IT - 1 and n == 2))
                mm.then_inc(xd_mm, 1)

            run_experts(pe, expert_step)
            pe.wait_ge(xo_up, 2 * NQ)

            def shared_step(v, it):
                if v < 88:
                    gate_up(v, it)
                if v > 22:
                    down(v - 1, it)

            run_shared(pe, shared_step)

        @block.scalar
        def _(act):
            def step(k, it):
                m = k % 8
                u = k + 1
                if within(u, NU):
                    wait(act, ct_mm, u + 1, 16, it)
                    act.copy(cT[:, HI].rearrange("p h n -> p (h n)"), c_bank[:, :]).then_inc(ct_hi, 1)
                u = k + 2
                if within(u, NU):
                    wait(act, pt_mm, u + 1, 16, it)
                    act.copy(pT[:, HI, :], t_bank[:, :]).then_inc(pt_hi, 1)
                u = k + 4
                if within(u, NU):
                    wait(act, maxed, u + 1, 16, it)
                    for h in range(4):
                        mm = act.activation(prob[:, u % 4, h, :], score_bank[u % 2][:, h * S:(h + 1) * S], ACT.Exp,
                                            bias=neg_max[:, u % 4, h:h + 1], accum_out=den[:, u % 4, h:h + 1])
                    mm.then_inc(exped, 1)
                q = k + 12
                if within(q, 8 * NG):
                    wait(act, pr_mm, q + 1, 16, it)
                    g, j = q // 8, q % 8
                    jp = slice(2 * (j // 2), 2 * (j // 2) + 2)
                    if j % 2 == 0:
                        act.copy(qT[g % 2][:, HI, jp, :],
                                 p_bank[:, :].rearrange("p (m n) -> p m n", m=2)).then_inc(pr_hi, 1)
                    else:
                        if q == 1:
                            act.wait_ge(kblk_zero, 2)
                        for s in range(2):
                            i = act.copy(kblk[g % 2][s * R:(s + 1) * R, HI, jp, :, s * S:(s + 1) * S],
                                         p_bank[s * R:(s + 1) * R, :].rearrange("p (m b n) -> p m b n", m=2, b=2))
                        i.then_inc(pr_hi, 1)
                if -8 <= k < 0:
                    for h in (2 * (k + 8), 2 * (k + 8) + 1):
                        act.wait_ge(m_mm, h + 1)
                        act.copy(M_w[:, HI, h, :], o_bank[h % 2][:, :]).then_inc(m_hi, 1)
                c = k // 8
                if m in (2, 3):
                    t1 = 2 * (c + 2) + m - 2
                    if within(t1, NB):
                        g = t1 // 2
                        wait(act, ln_mm["l1"], t1 + 1, 4, it)
                        wait(act, ln_lo["l1"], t1 - 1, 4, it)
                        wait(act, ln_lo["l2"], 2 * (c - 2) + m - 1, 4, it)
                        act.copy(xT32[:, t1 % 2, :], m_bank[:, :])
                        act.copy(xT1[g % 2][:, HI, :, (t1 % 2) * S:(t1 % 2 + 1) * S],
                                 m_bank[:, :].rearrange("p (t n) -> p t n", t=KT)).then_inc(ln_up["l1"], 1)
                if m in (4, 5):
                    b = 2 * (c - 1) + m - 4
                    if within(b, NB):
                        n = 2 * (c + 2) + m - 3
                        wait(act, ln_mm["l2"], b + 1, 4, it)
                        wait(act, ln_lo["l1"], min(n, NB) if it is None else n, 4, it)
                        wait(act, ln_lo["l2"], b - 1, 4, it)
                        wait(act, xT2_out[b % 2], 16 * (b // 2), 32, it)
                        act.copy(xT32[:, b % 2, :], m_bank[:, :])
                        act.copy(xT2[b % 2][:, HI].rearrange("p t n -> p (t n)"),
                                 m_bank[:, :]).then_inc(ln_up["l2"], 1)
                if m in (6, 7):
                    b = 2 * (c - 1) + m - 6
                    if within(b, NB):
                        wait(act, lg_mm, b + 1, 4, it)
                        act.copy(logits[:, b, :] if it is None else logits[:, bass.ds(at(b, 4, it), 1), :],
                                 m_bank[:, 0:E] if it is None else
                                 m_bank[:, 0:E].rearrange("p (o e) -> p o e", o=1)).then_inc(lg_up, 1)
                if it is None and within(k - FFN_FIRST, 12):
                    split_wsh(k - FFN_FIRST)

            def split_wsh(n):
                act.wait_ge(wsh_in[n % 3], 16 * (n // 3 + 1))
                act.copy(wsh[n // 2][:, HI, (n % 2) * PIECE:(n % 2 + 1) * PIECE], wsh_raw[:, n % 3, :])\
                    .then_inc(wsh_hi, 1)

            def split_wx(n, it):
                e, r = n // 4, n % 4
                wait(act, wx_in[n % 2], 16 * (n // 2 + 1), 64, it)
                if r == 0:
                    wait(act, xd_mm, 10 * (e - 1), 20, it)
                act.copy(wx[e % 2][:, HI, r * XPIECE:(r + 1) * XPIECE], wx_raw[:, n % 2, :]).then_inc(wx_hi, 1)

            act.wait_ge(const_in, 96)
            act.activation(tanh_sb, gate_sb, ACT.Tanh).then_inc(tanh_done, 1)
            for half in range(2):
                act.wait_ge(a_mm, half + 1)
                act.copy(A_sb[:, 8 * half:8 * half + 8, :].rearrange("p h r -> p (h r)"),
                         ab_bank[half][:, :]).then_inc(a_copied, 1)
            for n in range(8):
                act.wait_ge(b_mm, n + 1)
                act.copy(B_w[:, HI, n % KT, (n // KT) * 512:(n // KT + 1) * 512],
                         ab_bank[(n + 2) % 4][:, :]).then_inc(b_hi, 1)
            act.wait_ge(kr_in, 16)
            act.copy(Kr_w[:, HI, :], kr_stage).then_inc(kr_hi, 1)
            for k in range(FIRST_STEP, -12):
                step(k, None)
            run_steps(act, step)

            def silu_step(v, it):
                wait(act, gu_mm, v + 1, 22, it)
                act.activation(silu[v % 2], gate_bank[v % 2][:, :], ACT.Silu).then_inc(silu_done, 1)

            attention_over(act)
            act.wait_ge(gap_done, 1)
            act.activation(rt_exp, rt_gap, ACT.Exp).then_inc(exp_done, 1)
            for v in range(22):
                if v == 4:
                    act.wait_ge(ranked, 1)
                    act.copy(rt_rank, gate_bank[0][:, 0:N8])
                    act.copy(rt_count, gate_bank[0][:, N8:2 * N8]).then_inc(rank_up, 1)
                if v < 5:
                    split_wsh(12 + 2 * v)
                    split_wsh(13 + 2 * v)
                silu_step(v, None)
                if 16 <= v < 20:
                    split_wx(v - 16, None)

            def expert_step(k, it):
                for j in range(IT):
                    if within(k, NQ):
                        n1 = 3 * k + j
                        wait(act, xgu_mm, n1 + 1, 30, it)
                        act.activation(silu[n1 % 2][0:IW[j], 0:256], gu_bank[n1 % 2][0:IW[j], 0:256],
                                       ACT.Silu).then_inc(xsilu, 1)
                    if j == 0 and within(k + 1, NQ):
                        q = k + 1
                        wait(act, xt_mm, q + 1, 10, it)
                        for i in range(2):
                            act.copy(xgT[q % 2][:, HI, 2 * i:2 * i + 2, :].rearrange("p t n -> p (t n)"),
                                     xt_bank[i][:, :]).then_inc(xt_hi, 1)
                    if j == 1 and within(k - 1, NQ):
                        row_out(2 * (k - 1), it)
                if within(k - 1, NQ):
                    row_out(2 * (k - 1) + 1, it)
                e = (k + 4) // 5
                if 1 <= e < E and (k + 4) % 5 < 4:
                    split_wx(4 * e + (k + 4) % 5, it)

            def row_out(n1, it):
                wait(act, xd_mm, n1 + 1, 20, it)
                wait(act, xo_out[n1 % 4], 16 * (n1 // 4), 80, it)
                act.copy(xo[:, n1 % 4, :], xd_bank[n1 % 2][:, :]).then_inc(xo_up, 1)

            run_experts(act, expert_step)

            def shared_step(v, it):
                if v < 88:
                    silu_step(v, it)

            run_shared(act, shared_step)

        @block.vector
        def _(dve):
            def lower(dst, src, hi):
                return dve.tensor_tensor(dst, src, hi, ALU.subtract)

            def step(k, it):
                m = k % 8
                c = k // 8
                g2, g1 = c - 1, c + 2

                def links(*which):
                    if m in (0, 1) and (within(g2, NG) or within(g1, NG)):
                        for i in which:
                            rsqrt_link(i, g2, g1, it)

                u = k + 3
                if within(u, NU):
                    wait(dve, exped, u + 1, 16, it)
                    dve.reciprocal(rden[:, u % 4, :], den[:, u % 4, :]).then_inc(inverted, 1)
                links(*((1, 2) if m == 0 else (10, 11)))
                if k % 4 == 3 and within(k // 4, NB):
                    b = k // 4
                    wait(dve, o_mm, b + 1, 4, it)
                    wait(dve, xres_in[b % 2], 16 * (b // 2 + 1), 32, it)
                    if b == 0:
                        dve.wait_ge(tanh_done, 1)
                    dve.scalar_tensor_tensor(out=x1[:, b % 2, :], in0=o_bank[b % 2][:, :], scalar=tanh_sb[:, 0:1],
                                             in1=x1[:, b % 2, :], op0=ALU.mult, op1=ALU.add).then_inc(x1_done, 1)
                u = k + 1
                if within(u, NU):
                    wait(dve, ct_hi, u + 1, 16, it)
                    lower(cT[:, LO].rearrange("p h n -> p (h n)"), c_bank[:, :],
                          cT[:, HI].rearrange("p h n -> p (h n)")).then_inc(ct_lo, 1)
                links(*((3, 4) if m == 0 else (12, 13)))
                u = k + 2
                if within(u, NU):
                    wait(dve, pt_hi, u + 1, 16, it)
                    lower(pT[:, LO, :], t_bank[:, :], pT[:, HI, :]).then_inc(pt_lo, 1)
                links(*((5,) if m == 0 else (14,)))
                u = k + 4
                if within(u, NU):
                    wait(dve, scored, u + 1, 16, it)
                    dve.tensor_reduce(neg_max[:, u % 4, :], score_bank[u % 2][:, :].rearrange("p (h n) -> p h n", h=4),
                                      AX.X, ALU.max, negate=True).then_inc(maxed, 1)
                links(*((6, 7) if m == 0 else (15, 16)))
                q = k + 12
                if within(q, 8 * NG):
                    wait(dve, pr_hi, q + 1, 16, it)
                    g, j = q // 8, q % 8
                    jp = slice(2 * (j // 2), 2 * (j // 2) + 2)
                    if j % 2 == 0:
                        lower(qT[g % 2][:, LO, jp, :], p_bank[:, :].rearrange("p (m n) -> p m n", m=2),
                              qT[g % 2][:, HI, jp, :]).then_inc(pr_lo, 1)
                    else:
                        for s in range(2):
                            rows, cols = slice(s * R, (s + 1) * R), slice(s * S, (s + 1) * S)
                            i = lower(kblk[g % 2][rows, LO, jp, :, cols],
                                      p_bank[rows, :].rearrange("p (m b n) -> p m b n", m=2, b=2),
                                      kblk[g % 2][rows, HI, jp, :, cols])
                        i.then_inc(pr_lo, 1)
                links(*((8, 9) if m == 0 else (17,)))
                if m == 1:
                    norms(g2, g1, it)
                if -8 <= k < 0:
                    for h in (2 * (k + 8), 2 * (k + 8) + 1):
                        dve.wait_ge(m_hi, h + 1)
                        lower(M_w[:, LO, h, :], o_bank[h % 2][:, :], M_w[:, HI, h, :]).then_inc(m_lo, 1)
                if k % 4 == 3 and within(k // 4, NB):
                    b = k // 4
                    wait(dve, x1_done, b + 1, 4, it)
                    dve.bn_stats(stats[:, b % 2, :], x1[:, b % 2, :]).then_inc(stat2, 1)
                if m == 6 and within(c + 3, NG):
                    g = c + 3
                    wait(dve, xln_in, 16 * (g + 1), 32, it)
                    for s in range(2):
                        dve.bn_stats(stats[:, 2 + s, :], x_ln[:, s, :]).then_inc(stat1, 1)

            def rsqrt_link(i, g2, g1, it):
                has2, has1 = within(g2, NG), within(g1, NG)
                cols = slice(0 if has2 else 2, 4 if has1 else 2)
                v, y, n = var_eps[:, cols], rstd[:, cols], newton[:, cols]
                m_e, m_o, q_e, q_o = (stats[:, cols, f] for f in (1, 4, 2, 5))
                mu, dif = mean[:, cols], mean_dif[:, cols]
                if i == 1:
                    if has2:
                        wait(dve, stat2, 2 * g2 + 2, 4, it)
                    if has1:
                        wait(dve, stat1, 2 * g1 + 2, 4, it)
                    dve.tensor_tensor(mu, m_e, m_o, ALU.add)
                    dve.tensor_tensor(dif, m_e, m_o, ALU.subtract)
                    dve.tensor_tensor(v, q_e, q_o, ALU.add).then_inc(rsqrt_step, 1)
                    return
                wait(dve, rsqrt_step, RSQRT_OPS * g1 + i - 1, 2 * RSQRT_OPS, it)
                if i == 2:
                    dve.tensor_scalar(mu, mu, 0.5, None, ALU.mult)
                    dve.tensor_tensor(dif, dif, dif, ALU.mult)
                    ins = dve.tensor_scalar(v, v, 1.0 / D, EPS, ALU.mult, ALU.add)
                elif i == 3:
                    ins = dve.scalar_tensor_tensor(out=v, in0=dif, scalar=0.25, in1=v, op0=ALU.mult, op1=ALU.add)
                elif i == 4:
                    ins = dve.tensor_scalar(shifted[:, cols].bitcast(I32), v.bitcast(I32), 1, None,
                                            ALU.arith_shift_right)
                elif i == 5:
                    ins = dve.tensor_scalar(y.bitcast(I32), shifted[:, cols].bitcast(I32), -1.0, RSQRT_SEED,
                                            ALU.mult, ALU.add)
                elif i % 4 == 2:
                    ins = dve.tensor_tensor(n, v, y, ALU.mult)
                elif i % 4 == 3:
                    ins = dve.tensor_tensor(n, n, y, ALU.mult)
                elif i % 4 == 0:
                    ins = dve.tensor_scalar(n, n, -0.5, 1.5, ALU.mult, ALU.add)
                else:
                    ins = dve.tensor_tensor(y, y, n, ALU.mult)
                ins.then_inc(rsqrt_step, 1)

            def norms(g2, g1, it):
                if within(g2, NG) or within(g1, NG):
                    wait(dve, rsqrt_step, RSQRT_OPS * (g1 + 1), 2 * RSQRT_OPS, it)
                if within(g1, NG):
                    for s in range(2):
                        wait(dve, ln_mm["l1"], 2 * g1 + s - 1, 4, it)
                        dve.tensor_scalar(xn1[:, s, :], x_ln[:, s, :], mean[:, 2 + s:3 + s],
                                          rstd[:, 2 + s:3 + s], ALU.subtract, ALU.mult).then_inc(xn1_ready, 1)
                if within(g2, NG):
                    for s in range(2):
                        b = 2 * g2 + s
                        wait(dve, xn2_out[s], 16 * g2, 32, it)
                        wait(dve, ln_mm["l2"], b - 1, 4, it)
                        dve.tensor_scalar(xn2[:, s, :], x1[:, s, :], mean[:, s:s + 1], rstd[:, s:s + 1],
                                          ALU.subtract, ALU.mult).then_inc(xn2_ready, 1)

            for k in range(FIRST_STEP, -14):
                step(k, None)
            for n in range(8):
                dve.wait_ge(b_hi, n + 1)
                cols = slice((n // KT) * 512, (n // KT + 1) * 512)
                lower(B_w[:, LO, n % KT, cols], ab_bank[(n + 2) % 4][:, :], B_w[:, HI, n % KT, cols]).then_inc(b_lo, 1)
            dve.wait_ge(kr_hi, 1)
            lower(Kr_w[:, LO, :], kr_stage, Kr_w[:, HI, :]).then_inc(kr_lo, 1)
            for k in range(-14, -12):
                step(k, None)
            run_steps(dve, step)

            def hidden(v, it):
                wait(dve, silu_done, v + 1, 22, it)
                dve.tensor_tensor(h32[v % 2], silu[v % 2], up_bank[v % 2][:, :], ALU.mult).then_inc(h_mul, 1)
                wait(dve, h_mul, v + 1, 22, it)
                dve.tensor_copy(hsh[v % 2][:, HI, :], h32[v % 2]).then_inc(h_hi, 1)
                wait(dve, h_hi, v + 1, 22, it)
                lower(hsh[v % 2][:, LO, :], h32[v % 2], hsh[v % 2][:, HI, :]).then_inc(h_lo, 1)

            def add_shared(g, it):
                wait(dve, acc_mm, g + 1, 2, it)
                wait(dve, y_in, 16 * (g + 1 if it is None and g < 2 else g + 3), 32, it)
                for t in range(4):
                    dve.scalar_tensor_tensor(out=y_sb[:, t, :], in0=acc_bank[t][:, :], scalar=tanh_sb[:, 1:2],
                                             in1=y_sb[:, t, :], op0=ALU.mult, op1=ALU.add).then_inc(y_done, 1)

            def add_experts(t, it):
                i = t % 4
                wait(dve, r_in, 128 * (t // 4 + 1), 256, it)
                if t >= 8:
                    wait(dve, y_done, t + 1, 8, it)
                elif i == 0:
                    wait(dve, y_in, 16 * (t // 4 + 3), 0, None)
                for c, done in enumerate((comb_1, comb_2)):
                    dve.scalar_tensor_tensor(out=y_sb[:, i, :], in0=r_sb[:, 2 * i + c, :],
                                             scalar=weight_now[:, 2 * i + c:2 * i + c + 1], in1=y_sb[:, i, :],
                                             op0=ALU.mult, op1=ALU.add).then_inc(done, 1)
                    if c == 0:
                        wait(dve, comb_1, t + 1, 8, it)

            links = [0]

            def link(ins):
                links[0] += 1
                ins.then_inc(route_step, 1)
                dve.wait_ge(route_step, links[0])

            def tiles(v):
                return v.unsqueeze(2).broadcast_to([P, NB, E])

            def per(v):
                return v.rearrange("p (b e) -> p b e", e=E)

            def choose():
                ramp = route_sb[:, 2 * P:2 * P + E].unsqueeze(1).broadcast_to([P, NB, E])
                source = logits
                for c in range(2):
                    link(dve.tensor_reduce(rt_top[:, c, :], source, AX.X, ALU.max))
                    link(dve.tensor_tensor(per(rt_a), source, tiles(rt_top[:, c, :]), ALU.is_equal))
                    link(dve.tensor_tensor(per(rt_a), per(rt_a), ramp, ALU.mult))
                    link(dve.tensor_reduce(rt_rev[:, c, :], per(rt_a), AX.X, ALU.max))
                    link(dve.tensor_tensor(per(rt_hot[:, c, :]), ramp, tiles(rt_rev[:, c, :]), ALU.is_equal))
                    if c == 0:
                        link(dve.scalar_tensor_tensor(out=per(rt_b), in0=per(rt_hot[:, 0, :]), scalar=-3.0e38,
                                                      in1=logits, op0=ALU.mult, op1=ALU.add))
                        source = per(rt_b)
                dve.tensor_tensor(mask32, rt_hot[:, 0, :], rt_hot[:, 1, :], ALU.add).then_inc(masked, 1)
                dve.tensor_tensor(rt_gap, rt_top[:, 1, :], rt_top[:, 0, :], ALU.subtract).then_inc(gap_done, 1)
                dve.memset(rt_sum[:, 0, 0:P], 0.0)
                link(dve.memset(rt_sum[:, 1, 0:P], 0.0))

            def place():
                dve.wait_ge(rank_up, 1)
                link(dve.tensor_copy(rt_sum[:, 0, P:], rt_count))
                for i in range(5):
                    a, b = rt_sum[:, i % 2, :], rt_sum[:, (i + 1) % 2, :]
                    shift = E << i
                    link(dve.tensor_tensor(b[:, P:], a[:, P:], a[:, P - shift:P - shift + N8], ALU.add))
                link(dve.tensor_tensor(rt_a, rt_sum[:, 1, P:], rt_count, ALU.subtract))
                link(dve.tensor_tensor(rt_b, rt_a, rt_rank, ALU.add))
                dve.wait_ge(exp_done, 1)
                link(dve.tensor_scalar(rt_pos, rt_exp, 1.0, None, ALU.add))
                link(dve.reciprocal(rt_share[:, 0, :], rt_pos))
                link(dve.tensor_tensor(rt_share[:, 1, :], rt_share[:, 0, :], rt_exp, ALU.mult))

            def slots(c):
                link(dve.tensor_tensor(rt_a, rt_hot[:, c, :], rt_b, ALU.mult))
                link(dve.tensor_reduce(rt_pos, per(rt_a), AX.X, ALU.add))
                link(dve.tensor_scalar(rt_valid, rt_pos, float(CAP), None, ALU.is_lt))
                link(dve.tensor_scalar(rt_c, rt_rev[:, c, :], -float(CAP), float(E * CAP), ALU.mult, ALU.add))
                link(dve.tensor_tensor(rt_pos, rt_pos, rt_c, ALU.add))
                link(dve.tensor_tensor(rt_c, rt_pos, rt_valid, ALU.mult))
                link(dve.tensor_copy(slot_of[:, :, c], rt_c))
                link(dve.tensor_scalar(rt_c, rt_valid, -2.0 * E * CAP, 2.0 * E * CAP, ALU.mult, ALU.add))
                link(dve.tensor_tensor(rt_c, rt_c, rt_pos, ALU.add))
                link(dve.tensor_copy(scatter_to[:, :, c], rt_c))
                link(dve.tensor_scalar(rt_c, rt_share[:, c, :], tanh_sb[:, 1:2], None, ALU.mult))
                dve.tensor_tensor(weight_of[:, :, c], rt_c, rt_valid, ALU.mult).then_inc(routed, 1)
                dve.wait_ge(routed, c + 1)

            attention_over(dve)
            choose()
            for v in range(22):
                if v < 5:
                    for n in (12 + 2 * v, 13 + 2 * v):
                        dve.wait_ge(wsh_hi, n + 1)
                        cols = slice((n % 2) * PIECE, (n % 2 + 1) * PIECE)
                        lower(wsh[n // 2][:, LO, cols], wsh_raw[:, n % 3, :],
                              wsh[n // 2][:, HI, cols]).then_inc(wsh_lo, 1)
                hidden(v, None)
                if v == 5:
                    place()
                if v == 6:
                    slots(0)
                if v == 7:
                    slots(1)
                if v == 11:
                    add_shared(0, None)
            add_shared(1, None)

            def expert_step(k, it):
                for j in range(IT):
                    if within(k, NQ):
                        n1 = 3 * k + j
                        rows = slice(0, IW[j])
                        wait(dve, xsilu, n1 + 1, 30, it)
                        dve.tensor_tensor(h32[n1 % 2][rows, 0:256], silu[n1 % 2][rows, 0:256],
                                          gu_bank[n1 % 2][rows, 256:512], ALU.mult).then_inc(xmul, 1)
                        wait(dve, xmul, n1 + 1, 30, it)
                        dve.tensor_copy(hx[k % 2][rows, HI, j, :], h32[n1 % 2][rows, 0:256]).then_inc(xhh, 1)
                        wait(dve, xhh, n1 + 1, 30, it)
                        lower(hx[k % 2][rows, LO, j, :], h32[n1 % 2][rows, 0:256],
                              hx[k % 2][rows, HI, j, :]).then_inc(xhl, 1)
                    if j == 0 and within(k + 1, NQ):
                        q = k + 1
                        for i in range(2):
                            wait(dve, xt_hi, 2 * q + i + 1, 20, it)
                            lower(xgT[q % 2][:, LO, 2 * i:2 * i + 2, :].rearrange("p t n -> p (t n)"),
                                  xt_bank[i][:, :],
                                  xgT[q % 2][:, HI, 2 * i:2 * i + 2, :].rearrange("p t n -> p (t n)"))\
                                .then_inc(xt_lo, 1)

            run_experts(dve, expert_step)

            def shared_step(v, it):
                g, m = v // JT, v % JT
                if v < 88:
                    hidden(v, it)
                if m == 0 and g > 2:
                    add_shared(g - 1, it)
                if 24 <= v < 32:
                    add_experts(v - 24, None)
                if v >= 34 and 1 <= m <= 4:
                    add_experts(4 * (g - 1) + m - 1, it)

            run_shared(dve, shared_step)
            for t in range(28, 32):
                add_experts(t, None)

        @block.gpsimd
        def _(pool):
            tab = table_sb.rearrange("p (i n) -> p i n", i=4)

            def both(t):
                return tab[:, t, :].unsqueeze(1).broadcast_to([P, 2, P])

            def step(k, it):
                m = k % 8
                c = k // 8
                u = k + 3
                if within(u, NU):
                    wait(pool, inverted, u + 1, 16, it)
                    pool.tensor_tensor(prob[:, u % 4], prob[:, u % 4],
                                       rden[:, u % 4, :].unsqueeze(2).broadcast_to([P, 4, S]),
                                       ALU.mult).then_inc(normed, 1)
                if m in (4, 5):
                    b = 2 * (c - 1) + m - 4
                    if within(b, NB):
                        wait(pool, ln_up["l2"], b + 1, 4, it)
                        pool.tensor_tensor(xT2[b % 2][:, LO].rearrange("p t n -> p (t n)"), xT32[:, b % 2, :],
                                           xT2[b % 2][:, HI].rearrange("p t n -> p (t n)"),
                                           ALU.subtract).then_inc(ln_lo["l2"], 1)
                if m in (2, 3):
                    t1 = 2 * (c + 2) + m - 2
                    if within(t1, NB):
                        dst = xT1[(t1 // 2) % 2][:, :, :, (t1 % 2) * S:(t1 % 2 + 1) * S]
                        wait(pool, ln_up["l1"], t1 + 1, 4, it)
                        pool.tensor_tensor(dst[:, LO], xT32[:, t1 % 2, :].rearrange("p (t n) -> p t n", t=KT),
                                           dst[:, HI], ALU.subtract).then_inc(ln_lo["l1"], 1)
                if m == 0 and within(c + 2, NG):
                    g = c + 2
                    raw = kvT_raw.rearrange("p r (b n) -> p r b n", b=2)
                    a, b = (r.rearrange("p (b n) -> p b n", b=2) for r in (rope_a, rope_b))
                    base = 5 * g

                    def link(ins, i):
                        ins.then_inc(ropeT_step, 1)
                        wait(pool, ropeT_step, base + i, 10, it)

                    wait(pool, kvt_in, 16 * (g + 1), 32, it)
                    wait(pool, pr_mm, 8 * (g - 1), 16, it)
                    wait(pool, ropeN_step, max(6 * (g - 3) + 6, 0), 12, it)
                    link(pool.tensor_tensor(a, raw[:, 0], both(0), ALU.mult), 1)
                    link(pool.tensor_tensor(b, raw[:, 1], both(1), ALU.mult), 2)
                    link(pool.tensor_tensor(kvT[g % 2][:, HI, :], rope_a, rope_b, ALU.add), 3)
                    link(pool.tensor_tensor(a, a, b, ALU.add), 4)
                    link(pool.tensor_tensor(kvT[g % 2][:, LO, :], rope_a, kvT[g % 2][:, HI, :], ALU.subtract), 5)
                if m == 4 and within((k + 4) // 8, NG):
                    g = (k + 4) // 8
                    a, b = (r.rearrange("p (b n) -> p b n", b=2) for r in (rope_a, rope_b))
                    base = 6 * g

                    def link(ins, i):
                        ins.then_inc(ropeN_step, 1)
                        wait(pool, ropeN_step, base + i, 12, it)

                    wait(pool, kvn_in, 16 * (g + 1), 32, it)
                    wait(pool, ct_mm, 8 * (g - 1), 16, it)
                    hf = P // 2
                    link(pool.tensor_tensor(a, kvN_raw, both(2), ALU.mult), 1)
                    link(pool.tensor_tensor(b[:, :, 0:hf], kvN_raw[:, :, hf:P],
                                            tab[:, 3, 0:hf].unsqueeze(1).broadcast_to([P, 2, hf]), ALU.mult), 2)
                    link(pool.tensor_tensor(b[:, :, hf:P], kvN_raw[:, :, 0:hf],
                                            tab[:, 3, hf:P].unsqueeze(1).broadcast_to([P, 2, hf]), ALU.mult), 3)
                    link(pool.tensor_tensor(kvN[g % 2][:, HI], a, b, ALU.add), 4)
                    link(pool.tensor_tensor(a, a, b, ALU.add), 5)
                    link(pool.tensor_tensor(kvN[g % 2][:, LO], a, kvN[g % 2][:, HI], ALU.subtract), 6)
                if it is None and within(k - FFN_FIRST, 12):
                    lower_wsh(k - FFN_FIRST)

            def lower_wsh(n):
                pool.wait_ge(wsh_hi, n + 1)
                cols = slice((n % 2) * PIECE, (n % 2 + 1) * PIECE)
                pool.tensor_tensor(wsh[n // 2][:, LO, cols], wsh_raw[:, n % 3, :], wsh[n // 2][:, HI, cols],
                                   ALU.subtract).then_inc(wsh_lo, 1)

            pool.memset(zero_ids, 0).then_inc(zeroed, 1)
            pool.memset(one, 1.0).then_inc(zeroed, 1)
            pool.memset(k_region[:, 0:4096], 0.0).then_inc(kblk_zero, 1)
            pool.memset(k_region[:, 4096:8192], 0.0).then_inc(kblk_zero, 1)
            pool.wait_ge(zeroed, 2)
            pool.wait_ge(const_in, 96)
            for k in range(FIRST_STEP, -12):
                step(k, None)
            run_steps(pool, step)

            def wait_first(s, c, per, it, i):
                wait(pool, s, c, per, it)
                if it is not None:
                    pool.tensor_tensor(waited[:, i:i + 1], one, one, ALU.add)

            attention_over(pool)
            pool.wait_ge(routed, 2)
            pool.wait_ge(ids_zero, 16)
            for b in range(NB):
                for c in range(2):
                    pool.indirect_dma_start(
                        out=slot_token_d, out_offset=bass.IndirectOffsetOnAxis(ap=scatter_to[:, b, c:c + 1], axis=0),
                        in_=token_sb[:, b:b + 1], in_offset=None, bounds_check=E * CAP - 1,
                        oob_is_err=False).then_inc(scattered, 16)

            def lower_wx(n, it):
                e, cols = n // 4, slice((n % 4) * XPIECE, (n % 4 + 1) * XPIECE)
                wait(pool, wx_hi, n + 1, 8, it)
                pool.tensor_tensor(wx[e % 2][:, LO, cols], wx_raw[:, n % 2, :], wx[e % 2][:, HI, cols],
                                   ALU.subtract).then_inc(wx_lo, 1)

            for n in range(4):
                lower_wx(n, None)

            xn2_rows = xn2_d.rearrange("b s d -> (b s) d")

            def gather(q, it):
                e = q // 5
                if q % 5 == 0:
                    wait_first(ids_in[e % 2], 16 * (e // 2 + 1), 16, it, 10 + e % 2)
                wait_first(xt_mm, q - 1, 10, it, q % 10)
                for b in range(2):
                    i = 2 * (q % 5) + b
                    pool.indirect_dma_start(
                        out=xg[q % 2][:, b, :], out_offset=None, in_=xn2_rows,
                        in_offset=bass.IndirectOffsetOnAxis(ap=ids[:, e % 2, i:i + 1], axis=0))\
                        .then_inc(xg_in[q % 2], 16)

            def expert_step(k, it):
                if k == -1:
                    gather(0, None)
                if within(k + 2, NQ):
                    gather(k + 2, it)
                e = (k + 4) // 5
                if 1 <= e < E and (k + 4) % 5 < 4:
                    lower_wx(4 * e + (k + 4) % 5, it)

            run_experts(pool, expert_step)

            def gather_rows(s, it):
                wait_first(comb_2, 4 * s, 8, it, 12 + s % 2)
                cols = at(4 * s, 8, it)
                src = lambda v: (v[:, cols:cols + 4, :] if it is None else v[:, bass.ds(cols, 4), :])
                pool.tensor_copy(weight_now.rearrange("p (b c) -> p b c", c=2), src(weight_of))
                pool.tensor_copy(slot_now.rearrange("p (b c) -> p b c", c=2), src(slot_of)).then_inc(now_done, 1)
                wait_first(now_done, s + 1, 2, it, 14 + s % 2)
                for i in range(8):
                    pool.indirect_dma_start(out=r_sb[:, i, :], out_offset=None, in_=xrow_d,
                                            in_offset=bass.IndirectOffsetOnAxis(ap=slot_now[:, i:i + 1], axis=0))\
                        .then_inc(r_in, 16)

            def shared_step(v, it):
                g, m = v // JT, v % JT
                if v in (22, 28):
                    gather_rows(0 if v == 22 else 1, None)
                if v == 32:
                    gather_rows(2, None)
                if v >= 34 and m == 5 and g < 8:
                    gather_rows(g, it)

            pool.wait_ge(xd_mm, 2 * NQ)
            pool.wait_ge(xt_lo, 2 * NQ)
            for i in range(4):
                pool.wait_ge(xo_out[i], 16 * NQ // 2)
            run_shared(pool, shared_step)


def kernel(**inputs):
    import numpy as np
    import concourse.bacc as bacc
    from concourse.bass_utils import run_bass_kernel_spmd as run

    nc = bacc.Bacc("TRN2", target_bir_lowering=False, num_devices=1)
    f = {k: np.asarray(v) for k, v in inputs.items()}
    ctxt = f["ctx_512"].reshape(NG, 2, S, P)
    kv_t = ctxt.transpose(0, 3, 1, 2)
    kv_t = np.stack([kv_t, np.concatenate([kv_t[:, P // 2:], kv_t[:, :P // 2]], axis=1)], axis=2)
    inv = (np.float32(1.0) / np.float32(10000.0) ** (np.arange(0, P, 2, dtype=np.float32) / np.float32(P)))
    freq = np.arange(S, dtype=np.float32)[:, None] * inv[None, :].astype(np.float32)
    sin = np.repeat(np.sin(freq), 2, axis=-1).astype(np.float32)
    cos = np.repeat(np.cos(freq), 2, axis=-1).astype(np.float32)
    sin[:, :P // 2] *= -1
    gu = f["L0_ffn_shared_w_up_gate"].reshape(KT, P, 2, JT, P).transpose(3, 1, 0, 2, 4).reshape(JT, P, KT * 2 * P)
    w_shared = np.concatenate([gu, f["L0_ffn_shared_w_down"].reshape(JT, P, D)], axis=2)
    gu = f["L0_ffn_w_up_gate"].reshape(E, KT, P, 2 * I).transpose(0, 2, 1, 3).reshape(E, P, KT * 2 * I)
    dn = np.pad(f["L0_ffn_w_down"], ((0, 0), (0, IT * P - I), (0, 0)))
    dn = dn.reshape(E, IT, P, D).transpose(0, 2, 1, 3).reshape(E, P, IT * D)
    w_expert = np.concatenate([gu, dn], axis=2)
    arrays = {
        "x": f["x"],
        "kv_t": np.ascontiguousarray(kv_t.reshape(NG, P, 2, 2 * S)),
        "kv_n": np.ascontiguousarray(ctxt.transpose(0, 2, 1, 3)),
        "gates": np.ascontiguousarray(np.broadcast_to(np.concatenate([f["g_xattn"], f["g_ffn"]]), (P, 2))),
        "Wq": f["L0_xattn_Wq"],
        "w_qk": np.ascontiguousarray(f["L0_xattn_w_kc_q"].transpose(2, 0, 1).reshape(DQ, H * P)),
        "W_qr": np.ascontiguousarray(f["L0_xattn_W_qr"].transpose(1, 0, 2).reshape(DQ, H * R)),
        "W_kr": np.ascontiguousarray(f["L0_xattn_W_kr"].transpose(1, 0, 2).reshape(P, H * R)),
        "w_kv": f["L0_xattn_w_kc_kv"],
        "Wo_t": np.ascontiguousarray(f["L0_xattn_Wo"].T),
        "router": f["L0_ffn_router"],
        "tables": np.concatenate([cos.T, sin.T, cos, sin], axis=1).astype(np.float32),
        "ident": np.eye(P, dtype=np.float32),
        "w_shared": w_shared,
        "w_expert": w_expert,
        "route_const": np.concatenate([np.triu(np.ones((P, P)), 1), np.ones((P, P)),
                                       np.broadcast_to(E - np.arange(E), (P, E))], axis=1).astype(np.float32),
        "token_ids": (np.arange(NB)[None, :] * P + np.arange(P)[:, None]).astype(np.int32),
    }
    args = [nc.dram_tensor(k, a.shape, mybir.dt.from_np(a.dtype), kind="ExternalInput").ap()
            for k, a in arrays.items()]
    out = nc.dram_tensor("result", (NB, S, D), F32, kind="ExternalOutput").ap()
    build(nc, *args, out)
    r = run(nc, [arrays], core_ids=[0])
    return r.results[0]["result"]
```

```python
from contextlib import ExitStack

import concourse.bass as bass
from concourse import mybir

F32 = mybir.dt.float32
BF16 = mybir.dt.bfloat16
I32 = mybir.dt.int32
ALU = mybir.AluOpType
ACT = mybir.ActivationFunctionType
AX = mybir.AxisListType

P = 128
NB = 32
S = 128
D = 512
KT = D // P
H = 16
R = 64
DQ = 384
NPAIR = H // 2
UPB = 4
NU = NB * UPB
NG = NB // 2
EPS = 1e-5
RSQRT_SEED = float(0x5F3759DF)
RSQRT_OPS = 17

E = 8
I = 352
CAP = 1280
J = 1408
JT = J // P
SLICE = KT * 2 * P + D
PIECE = SLICE // 2
IT = 3
IW = [P, P, I - 2 * P]
XW = KT * 2 * I + IT * D
XPIECE = XW // 4
TPX = CAP // P
NQ = E * TPX // 2

HI, LO = 0, 1
PASSES = ((HI, HI), (HI, LO), (LO, HI))

FIRST_STEP, LOOP_STEP, LOOPS, LAST_STEP = -24, 16, 5, 135
FFN_FIRST = 98
BODY = 16


def build(nc, x, kv_t, kv_n, gates, Wq, w_qk, W_qr, W_kr, w_kv, Wo_t, router, tables, ident, w_shared, w_expert,
          route_const, token_ids, out):
    ctx = ExitStack()
    with ctx:
        def sem(name):
            return ctx.enter_context(nc.semaphore(name))

        def bank(name):
            return ctx.enter_context(nc.psum_tensor(name, [P, 512], F32))

        ARENA = 52900
        arena = ctx.enter_context(nc.sbuf_tensor("arena", [P, ARENA], F32))
        taken = [0]

        def words(n):
            at = taken[0]
            taken[0] += n
            assert taken[0] <= ARENA, taken[0]
            return arena[:, at:at + n]

        def halves(region):
            return region.bitcast(BF16)

        ident_sb = words(P)
        table_sb = words(4 * P)
        router_sb = words(KT * E)
        gate_sb = words(2)
        tanh_sb = words(2)
        route_sb = words(2 * P + E)
        token_sb = words(NB).bitcast(I32)
        one, waited = words(1), words(16)
        zero_ids = words(E * CAP // P).bitcast(I32)
        logits = words(NB * E).rearrange("p (b e) -> p b e", e=E)
        slot_of = words(2 * NB).bitcast(I32).rearrange("p (b c) -> p b c", c=2)
        scatter_to = words(2 * NB).bitcast(I32).rearrange("p (b c) -> p b c", c=2)
        weight_of = words(2 * NB).rearrange("p (b c) -> p b c", c=2)

        bm_at = taken[0]
        B_region = words(2 * KT * H * R // 2)
        B_w = halves(B_region).rearrange("p (l t n) -> p l t n", l=2, t=KT)
        M_region = words(2 * H * D // 2)
        M_w = halves(M_region).rearrange("p (l h n) -> p l h n", l=2, h=H)
        BM_region = arena[:, bm_at:taken[0]]
        k_region = words(2 * NPAIR * 512)
        work_at = taken[0]
        Kr_w = halves(words(H * R)).rearrange("p (l n) -> p l n", l=2)
        q_region = words(2 * NPAIR * 256)
        qT = [halves(q_region[:, g * 2048:(g + 1) * 2048]).rearrange("p (l m n) -> p l m n", l=2, m=NPAIR)
              for g in range(2)]
        kblk = [halves(k_region[:, g * 4096:(g + 1) * 4096]).rearrange("p (l m b n) -> p l m b n", l=2, m=NPAIR, b=2)
                for g in range(2)]
        xT1_region = words(2 * KT * 256)
        xT1 = [halves(xT1_region[:, g * 1024:(g + 1) * 1024]).rearrange("p (l t n) -> p l t n", l=2, t=KT)
               for g in range(2)]
        kvT_region = words(2 * 256)
        kvT = [halves(kvT_region[:, g * 256:(g + 1) * 256]).rearrange("p (l n) -> p l n", l=2) for g in range(2)]
        kvN_region = words(2 * 256)
        kvN = [halves(kvN_region[:, g * 256:(g + 1) * 256]).rearrange("p (l b n) -> p l b n", l=2, b=2)
               for g in range(2)]
        kvT_raw = words(512).rearrange("p (r n) -> p r n", r=2)
        kvN_raw = words(256).rearrange("p (b n) -> p b n", b=2)
        rope_a = words(256)
        rope_b = words(256)
        prob_region = words(4 * 512)
        prob = prob_region.rearrange("p (u h n) -> p u h n", u=4, h=4)
        kr_at = taken[0]
        pT_region = words(512)
        pT = halves(pT_region).rearrange("p (l n) -> p l n", l=2)
        cT_region = words(512)
        cT = halves(cT_region).rearrange("p (l h n) -> p l h n", l=2, h=4)
        neg_max = words(16).rearrange("p (u h) -> p u h", u=4)
        den = words(16).rearrange("p (u h) -> p u h", u=4)
        rden = words(16).rearrange("p (u h) -> p u h", u=4)
        x_ln = words(2 * D).rearrange("p (b n) -> p b n", b=2)
        xn1 = words(2 * D).rearrange("p (b n) -> p b n", b=2)
        x1 = words(2 * D).rearrange("p (b n) -> p b n", b=2)
        factor_at = taken[0]
        xn2 = words(2 * D).rearrange("p (b n) -> p b n", b=2)
        xT32 = words(2 * D).rearrange("p (b n) -> p b n", b=2)
        xT2 = [halves(words(D)).rearrange("p (l t n) -> p l t n", l=2, t=KT) for _ in range(2)]
        stats = words(4 * 6).rearrange("p (c n) -> p c n", c=4)
        mean = words(4)
        mean_dif = words(4)
        var_eps = words(4)
        shifted = words(4)
        rstd = words(4)
        newton = words(4)
        work_region = arena[:, work_at:taken[0]]
        stage = words(2 * H * (D // 2 + 32))
        wqk_sb = stage[:, 0:3 * H * P].rearrange("p (t h k) -> p t h k", t=3, h=H)
        wqr_sb = stage[:, 3 * H * P:3 * H * (P + R)].rearrange("p (t h r) -> p t h r", t=3, h=H)
        Wq_sb = M_region.rearrange("p (h d) -> p h d", h=H)
        A_w = halves(prob_region[:, 0:H * R]).rearrange("p (l h r) -> p l h r", l=2, h=H)
        Wq_w = [halves(r).rearrange("p (l h d) -> p l h d", l=2, h=H // 2) for r in (k_region[:, 4096:], stage[:, 0:4096])]
        assert pT_region.shape == cT_region.shape
        kr_stage = arena[:, kr_at:kr_at + H * R]
        wo_wkv = words(4 * (D + P))
        mf_ring = wo_wkv.rearrange("p (s n) -> p s n", s=4)
        assert factor_at + 4 * (D + P) <= taken[0]
        mf_w = halves(arena[:, factor_at:factor_at + 4 * (D + P)]).rearrange("p (s l n) -> p s l n", s=4, l=2)


        wsh_raw = wo_wkv[:, 0:3 * PIECE].rearrange("p (s n) -> p s n", s=3)
        wsh = [halves(stage[:, i * SLICE:(i + 1) * SLICE]).rearrange("p (l n) -> p l n", l=2) for i in range(6)]
        wsh += [halves(k_region[:, i * SLICE:(i + 1) * SLICE]).rearrange("p (l n) -> p l n", l=2) for i in range(5)]
        wx = [halves(BM_region[:, i * XW:(i + 1) * XW]).rearrange("p (l n) -> p l n", l=2) for i in range(2)]
        spare = [BM_region[:, 2 * XW:], work_region]
        used = [0, 0]

        def reuse(n, r=1):
            at = used[r]
            used[r] += n
            assert used[r] <= spare[r].shape[1], (used, spare[r].shape)
            return spare[r][:, at:at + n]

        wx_raw = reuse(2 * XPIECE, 0).rearrange("p (s n) -> p s n", s=2)
        xs = [halves(reuse(4 * D)).rearrange("p (b n) -> p b n", b=4) for _ in range(2)]
        hsh = [halves(reuse(512)).rearrange("p (l n) -> p l n", l=2) for _ in range(2)]
        silu = [reuse(512) for _ in range(2)]
        h32 = [reuse(512) for _ in range(2)]
        y_sb = reuse(4 * D).rearrange("p (b n) -> p b n", b=4)
        either = reuse(8 * D)
        r_sb = either.rearrange("p (r n) -> p r n", r=8)
        xg = [either[:, i * 1024:(i + 1) * 1024].rearrange("p (b n) -> p b n", b=2) for i in range(2)]
        xgT = [halves(either[:, 2048 + i * 1024:3072 + i * 1024]).rearrange("p (l t n) -> p l t n", l=2, t=KT)
               for i in range(2)]
        hx = [halves(reuse(IT * 256)).rearrange("p (l j n) -> p l j n", l=2, j=IT) for _ in range(2)]
        xo = reuse(4 * D).rearrange("p (s n) -> p s n", s=4)
        ids = reuse(2 * TPX).bitcast(I32).rearrange("p (s n) -> p s n", s=2)
        slot_now = reuse(8).bitcast(I32)
        weight_now = reuse(8)
        N8 = NB * E
        mask32, rt_a, rt_b, rt_rank, rt_count = (either[:, i * N8:(i + 1) * N8] for i in range(5))
        rt_hot = either[:, 5 * N8:7 * N8].rearrange("p (c n) -> p c n", c=2)
        rt_sum = either[:, 7 * N8:7 * N8 + 2 * (P + N8)].rearrange("p (c n) -> p c n", c=2)
        small = either[:, 10 * N8:10 * N8 + 10 * NB]
        rt_top, rt_rev, rt_share = (small[:, 2 * i * NB:2 * (i + 1) * NB].rearrange("p (c n) -> p c n", c=2)
                                    for i in range(3))
        rt_gap, rt_exp, rt_pos, rt_valid = (small[:, (6 + i) * NB:(7 + i) * NB] for i in range(4))
        rt_c = either[:, 11 * N8 + 2 * NB:11 * N8 + 3 * NB]

        score_bank = [bank("score0"), bank("score1")]
        t_bank = bank("t_bank")
        c_bank = bank("c_bank")
        o_bank = [bank("o0"), bank("o1")]
        p_bank = bank("p_bank")
        m_bank = bank("m_bank")
        ab_bank = [score_bank[0], score_bank[1], o_bank[0], o_bank[1]]

        def piece_bank(q):
            return score_bank[1] if q % 2 == 1 and q < 8 else p_bank

        acc_bank = [o_bank[0], o_bank[1], t_bank, c_bank]
        gate_bank = [score_bank[0], p_bank]
        up_bank = [score_bank[1], m_bank]
        xt_bank = [t_bank, c_bank]
        gu_bank = [score_bank[0], score_bank[1]]
        xd_bank = [o_bank[0], o_bank[1]]

        x1_d = nc.dram_tensor("x1_d", [NB, S, D], F32, kind="Internal").ap()
        xn2_d = nc.dram_tensor("xn2_d", [NB, S, D], F32, kind="Internal").ap()
        xT2_d = nc.dram_tensor("xT2_d", [NB, P, 2 * D], BF16, kind="Internal").ap()
        y_d = nc.dram_tensor("y_d", [8, S, D], F32, kind="Internal").ap()
        slot_token_d = nc.dram_tensor("slot_token_d", [E * CAP, 1], I32, kind="Internal").ap()
        xrow_d = nc.dram_tensor("xrow_d", [E * CAP, D], F32, kind="Internal").ap()

        const_in, table_in = sem("const_in"), sem("table_in")
        wa_in = [sem(f"wa_in{i}") for i in range(4)]
        wq_in = [sem(f"wq_in{i}") for i in range(4)]
        kr_in = sem("kr_in")
        wo_in = [sem(f"wo_in{i}") for i in range(4)]
        a_mm, a_hi, a_lo, b_mm, b_hi, b_lo = sem("a_mm"), sem("a_hi"), sem("a_lo"), sem("b_mm"), sem("b_hi"), sem("b_lo")
        kr_hi, kr_lo = sem("kr_hi"), sem("kr_lo")
        wq_hi, wq_lo = sem("wq_hi"), [sem("wq_lo_even"), sem("wq_lo_odd")]
        mf_hi, mf_lo = sem("mf_hi"), sem("mf_lo")
        m_mm, m_hi, m_lo = sem("m_mm"), sem("m_hi"), sem("m_lo")
        tanh_done, kblk_zero = sem("tanh_done"), sem("kblk_zero")
        xln_in, kvt_in, kvn_in = sem("xln_in"), sem("kvt_in"), sem("kvn_in")
        xres_in = [sem("xres_in0"), sem("xres_in1")]
        x1_out = [sem("x1_out0"), sem("x1_out1")]
        xn2_out = [sem("xn2_out0"), sem("xn2_out1")]
        xT2_out = [sem("xT2_out0"), sem("xT2_out1")]
        scored, maxed, exped, inverted, normed = (sem("scored"), sem("maxed"), sem("exped"), sem("inverted"),
                                                  sem("normed"))
        pt_mm, pt_hi, pt_lo = sem("pt_mm"), sem("pt_hi"), sem("pt_lo")
        ct_mm, ct_hi, ct_lo = sem("ct_mm"), sem("ct_hi"), sem("ct_lo")
        o_mm, x1_done = sem("o_mm"), sem("x1_done")
        pr_mm, pr_hi, pr_lo = sem("pr_mm"), sem("pr_hi"), sem("pr_lo")
        ln_mm = {"l1": sem("l1_mm"), "l2": sem("l2_mm")}
        ln_up = {"l1": sem("l1_up"), "l2": sem("l2_up")}
        ln_lo = {"l1": sem("l1_lo"), "l2": sem("l2_lo")}
        lg_mm, lg_up = sem("lg_mm"), sem("lg_up")
        stat1, stat2 = sem("stat1"), sem("stat2")
        rsqrt_step, xn1_ready, xn2_ready = sem("rsqrt_step"), sem("xn1_ready"), sem("xn2_ready")
        ropeT_step, ropeN_step = sem("ropeT_step"), sem("ropeN_step")

        wsh_in = [sem(f"wsh_in{i}") for i in range(3)]
        wsh_hi, wsh_lo = sem("wsh_hi"), sem("wsh_lo")
        xs_in = [sem("xs_in0"), sem("xs_in1")]
        y_in, y_out = sem("y_in"), sem("y_out")
        gu_mm, silu_done, h_mul, h_hi, h_lo = sem("gu_mm"), sem("silu_done"), sem("h_mul"), sem("h_hi"), sem("h_lo")
        acc_mm, y_done, comb_1, comb_2 = sem("acc_mm"), sem("y_done"), sem("comb_1"), sem("comb_2")
        route_step, masked, ranked, rank_up = sem("route_step"), sem("masked"), sem("ranked"), sem("rank_up")
        gap_done, exp_done, routed = sem("gap_done"), sem("exp_done"), sem("routed")
        zeroed, ids_zero, scattered = sem("zeroed"), sem("ids_zero"), sem("scattered")
        ids_in = [sem("ids_in0"), sem("ids_in1")]
        wx_in = [sem("wx_in0"), sem("wx_in1")]
        wx_hi, wx_lo = sem("wx_hi"), sem("wx_lo")
        xg_in = [sem("xg_in0"), sem("xg_in1")]
        xt_mm, xt_hi, xt_lo = sem("xt_mm"), sem("xt_hi"), sem("xt_lo")
        xgu_mm, xsilu, xmul, xhh, xhl = sem("xgu_mm"), sem("xsilu"), sem("xmul"), sem("xhh"), sem("xhl")
        xd_mm, xo_up = sem("xd_mm"), sem("xo_up")
        xo_out = [sem(f"xo_out{i}") for i in range(4)]
        now_done, r_in = sem("now_done"), sem("r_in")

        block = ctx.enter_context(nc.Block())

        def wait(eng, s, c, per, it):
            if it is None:
                if c > 0:
                    eng.wait_ge(s, c)
            else:
                assert c > 0
                eng.wait_ge(s, it * per + c)

        def at(c, per, it):
            return c if it is None else it * per + c

        def run_steps(eng, step, last=LAST_STEP):
            for k in range(-12, LOOP_STEP):
                step(k, None)
            with eng.Fori(0, LOOPS) as it:
                for k in range(LOOP_STEP, LOOP_STEP + BODY):
                    step(k, it)
            for k in range(LOOP_STEP + BODY * LOOPS, last + 1):
                step(k, None)

        def within(i, n):
            return 0 <= i < n

        def run_shared(eng, step):
            for v in range(22, 33):
                step(v, None)
            with eng.Fori(0, 2) as it:
                for v in range(33, 55):
                    step(v, it)
            for v in range(77, 89):
                step(v, None)

        def run_experts(eng, step, first=-1):
            for k in range(first, 3):
                step(k, None)
            with eng.Fori(0, 3) as it:
                for k in range(3, 13):
                    step(k, it)
            for k in range(33, NQ + 1):
                step(k, None)

        def attention_over(eng):
            for s, c in ((o_mm, NB), (x1_done, NB), (lg_mm, NB), (lg_up, NB), (xn2_ready, NB), (ln_lo["l2"], NB),
                         (ropeN_step, 6 * NG)):
                eng.wait_ge(s, c)
            for p in range(2):
                for s in (x1_out, xn2_out, xT2_out):
                    eng.wait_ge(s[p], 16 * NB // 2)

        @block.sync
        def _(sp):
            def step(k, it):
                m = k % 8
                if m == 1:
                    g = (k + 23) // 8
                    if within(g, NG):
                        wait(sp, ropeT_step, 5 * g, 10, it)
                        sp.dma_start(kvT_raw, kv_t[at(g, 2, it)]).then_inc(kvt_in, 16)
                if m == 5:
                    g = (k + 11) // 8
                    if within(g, NG):
                        wait(sp, ropeN_step, 6 * g, 12, it)
                        sp.dma_start(kvN_raw, kv_n[at(g, 2, it)]).then_inc(kvn_in, 16)
                if k % 4 == 0 and within(k // 4 - 1, NB):
                    b = k // 4 - 1
                    wait(sp, x1_done, b + 1, 4, it)
                    sp.dma_start(x1_d[at(b, 4, it)], x1[:, b % 2, :]).then_inc(x1_out[b % 2], 16)
                if m == 2:
                    g = (k + 22) // 8
                    if within(g, NG):
                        wait(sp, xn1_ready, 2 * g, 4, it)
                        sp.dma_start(x_ln, x_g[at(g, 2, it)]).then_inc(xln_in, 16)
                    g = k // 8 - 1
                    for b in (2 * g, 2 * g + 1):
                        if within(b, NB):
                            wait(sp, xn2_ready, b + 1, 4, it)
                            sp.dma_start(xn2_d[at(b, 4, it)], xn2[:, b % 2, :]).then_inc(xn2_out[b % 2], 16)
                    for b in (2 * g + 2, 2 * g + 3):
                        if within(b, NB):
                            wait(sp, x1_out[b % 2], 16 * (b // 2), 32, it)
                            wait(sp, xn2_ready, b - 1, 4, it)
                            sp.dma_start(x1[:, b % 2, :], x[at(b, 4, it)]).then_inc(xres_in[b % 2], 16)
                if m in (6, 7):
                    b = 2 * (k // 8 - 1) + m - 6
                    if within(b, NB):
                        wait(sp, ln_lo["l2"], b + 1, 4, it)
                        sp.dma_start(xT2_d[at(b, 4, it)],
                                     xT2[b % 2].rearrange("p l t n -> p (l t n)")).then_inc(xT2_out[b % 2], 16)
                if -12 <= k < -8:
                    load_m(2 * (k + 12) + 8)
                    load_m(2 * (k + 12) + 9)
                if it is None and within(k - FFN_FIRST + 1, 12):
                    load_wsh(k - FFN_FIRST + 1)

            x_g = x.rearrange("(g b) s d -> g s b d", b=2)
            wo_h = Wo_t.rearrange("(h k) n -> h k n", h=H)

            def load_m(h):
                wait(sp, mf_lo, h - 3, 0, None)
                sp.dma_start(mf_ring[:, h % 4, 0:D], wo_h[h]).then_inc(wo_in[h % 4], 16)
                sp.dma_start(mf_ring[:, h % 4, D:], w_kv[h]).then_inc(wo_in[h % 4], 16)

            def load_wsh(n):
                sp.wait_ge(m_mm, H)
                wait(sp, wsh_lo, n - 2, 0, None)
                sp.dma_start(wsh_raw[:, n % 3, :], w_shared[n // 2, :, (n % 2) * PIECE:(n % 2 + 1) * PIECE])\
                    .then_inc(wsh_in[n % 3], 16)

            def load_wx(n, it):
                wait(sp, wx_lo, n - 1, 8, it)
                sp.dma_start(wx_raw[:, n % 2, :], w_x[at(n // 4, 2, it), n % 4]).then_inc(wx_in[n % 2], 16)

            w_x = w_expert.rearrange("e p (r n) -> e r p n", r=4)
            w_qk4 = w_qk.rearrange("(t p) (c n) -> c p t n", t=3, c=4)
            W_qr4 = W_qr.rearrange("(t p) (c n) -> c p t n", t=3, c=4)

            def load_a(c):
                heads = slice(4 * c, 4 * c + 4)
                sp.dma_start(wqk_sb[:, :, heads, :].rearrange("p t h k -> p t (h k)"), w_qk4[c]).then_inc(wa_in[c], 16)
                sp.dma_start(wqr_sb[:, :, heads, :].rearrange("p t h r -> p t (h r)"), W_qr4[c]).then_inc(wa_in[c], 16)

            load_a(0)
            step(-22, None)
            load_a(1)
            step(-23, None)
            sp.dma_start(ident_sb, ident).then_inc(table_in, 16)
            sp.dma_start(table_sb, tables).then_inc(table_in, 16)
            load_a(2)
            load_a(3)
            Wq_h = Wq.rearrange("(h k) d -> k h d", h=H)
            for c in range(4):
                heads = slice(4 * c, 4 * c + 4)
                sp.dma_start(Wq_sb[:, heads, :], Wq_h[:, heads, :]).then_inc(wq_in[c], 16)
            sp.dma_start(kr_stage, W_kr).then_inc(kr_in, 16)
            sp.dma_start(route_sb, route_const).then_inc(const_in, 16)
            sp.dma_start(token_sb, token_ids).then_inc(const_in, 16)
            sp.dma_start(gate_sb, gates).then_inc(const_in, 16)
            sp.dma_start(router_sb.rearrange("p (t e) -> p t e", t=KT),
                         router.rearrange("(t p) e -> p t e", t=KT)).then_inc(const_in, 16)
            for h in range(4):
                load_m(h)
            for k in range(-21, -12):
                step(k, None)
            sp.wait_ge(zeroed, 2)
            sp.dma_start(slot_token_d.rearrange("(p c) o -> p (c o)", p=P), zero_ids).then_inc(ids_zero, 16)
            xT2_g = xT2_d.rearrange("(g b) p n -> g p b n", b=4)
            for h in range(4, 8):
                load_m(h)
            run_steps(sp, step, NU - 2)
            sp.wait_ge(scored, NU)
            sp.dma_start(xs[0], xT2_g[0]).then_inc(xs_in[0], 16)
            for k in range(NU - 1, LAST_STEP + 1):
                step(k, None)

            x1_t = x1_d.rearrange("(g b) s d -> g s b d", b=4)
            y_t = y_d.rearrange("(g b) s d -> g s b d", b=4)
            attention_over(sp)
            sp.dma_start(xs[1], xT2_g[1]).then_inc(xs_in[1], 16)
            sp.dma_start(y_sb, x1_t[0]).then_inc(y_in, 16)
            for n in range(12, 2 * JT):
                load_wsh(n)
            sp.wait_ge(gu_mm, 11)
            sp.dma_start(xs[0], xT2_g[2]).then_inc(xs_in[0], 16)
            for t in range(4):
                sp.wait_ge(y_done, t + 1)
                sp.dma_start(y_d[t], y_sb[:, t, :]).then_inc(y_out, 16)
            sp.wait_ge(y_out, 64)
            sp.dma_start(y_sb, x1_t[1]).then_inc(y_in, 16)
            for r in range(4):
                load_wx(r, None)

            def load_ids(e, it):
                wait(sp, xt_mm, 5 * (e - 1), 10, it)
                sp.dma_start(ids[:, e % 2, :], ids_e[at(e, 2, it)]).then_inc(ids_in[e % 2], 16)

            ids_e = slot_token_d.rearrange("(e p c) o -> e p (c o)", e=E, p=P)
            sp.wait_ge(scattered, 64 * 16)
            load_ids(0, None)
            for t in range(4):
                sp.wait_ge(y_done, 4 + t + 1)
                sp.dma_start(y_d[4 + t], y_sb[:, t, :]).then_inc(y_out, 16)

            xrow_v = xrow_d.rearrange("(e p c) d -> e c p d", e=E, p=P)

            def expert_step(k, it):
                e = (k + 5) // 5
                if e >= 1 and e < E and k % 5 == 0:
                    load_ids(e, it)
                if 1 <= e < E and k % 5 < 4:
                    load_wx(4 * e + k % 5, it)
                q = k - 1
                if within(q, NQ):
                    for t in range(2):
                        n = 2 * q + t
                        wait(sp, xo_up, n + 1, 20, it)
                        sp.dma_start(xrow_v[at(q // 5, 2, it), 2 * (q % 5) + t], xo[:, n % 4, :])\
                            .then_inc(xo_out[n % 4], 16)

            sp.wait_ge(gu_mm, 22)
            sp.dma_start(xs[1], xT2_g[3]).then_inc(xs_in[1], 16)
            sp.wait_ge(y_out, 16 * 8)
            sp.dma_start(y_sb, y_t[0]).then_inc(y_in, 16)
            run_experts(sp, expert_step)

            def shared_step(v, it):
                g, m = v // JT, v % JT
                if v in (28, 32):
                    sp.wait_ge(y_out, 16 * (12 if v == 28 else 16))
                    sp.dma_start(y_sb, y_t[1] if v == 28 else x1_t[2]).then_inc(y_in, 16)
                if 24 <= v < 32:
                    t = v - 24
                    store_out(t, t, None)
                if v >= 34 and 1 <= m <= 4:
                    t = 4 * (g - 1) + m - 1
                    store_out(t, t, it)
                if v >= 34 and m == 5 and g < 8:
                    wait(sp, y_out, 16 * 4 * (g + 2), 128, it)
                    sp.dma_start(y_sb, x1_t[at(g, 2, it)]).then_inc(y_in, 16)
                if m == 0 and 3 <= g < 7:
                    wait(sp, gu_mm, 11 * g, 22, it)
                    sp.dma_start(xs[(g + 1) % 2], xT2_g[at(g + 1, 2, it)]).then_inc(xs_in[(g + 1) % 2], 16)

            def store_out(t, c, it):
                wait(sp, comb_2, c + 1, 8, it)
                sp.dma_start(out[at(t, 8, it)], y_sb[:, t % 4, :]).then_inc(y_out, 16)

            run_shared(sp, shared_step)
            for t in range(28, 32):
                sp.wait_ge(y_done, t + 1)
                sp.dma_start(out[t], y_sb[:, t % 4, :]).then_inc(y_out, 16)
            sp.wait_ge(y_out, 16 * 40)

        @block.tensor
        def _(pe):
            def step(k, it):
                m = k % 8
                u = k
                if within(u, NU):
                    b, hg = u // 4, u % 4
                    wait(pe, ct_lo, u + 1, 16, it)
                    if hg == 0:
                        wait(pe, x1_done, b - 1, 4, it)
                        if u == 0:
                            pe.wait_ge(m_lo, H)
                    n = 0
                    for h in range(4):
                        for a, w in PASSES:
                            mm = pe.matmul(o_bank[b % 2][:, :], lhsT=cT[:, a, h, :], rhs=M_w[:, w, 4 * hg + h, :],
                                           start=(hg == 0 and n == 0), stop=(hg == 3 and n == 11))
                            n += 1
                    if hg == 3:
                        mm.then_inc(o_mm, 1)
                u = k + 1
                if within(u, NU):
                    g, b = u // 8, u // 4
                    wait(pe, pt_lo, u + 1, 16, it)
                    wait(pe, ct_lo, u, 16, it)
                    if u % 8 == 0:
                        wait(pe, ropeN_step, 6 * (g + 1), 12, it)
                    for n, (a, w) in enumerate(PASSES):
                        mm = pe.matmul(c_bank[:, :], lhsT=kvN[g % 2][:, a, b % 2, :], rhs=pT[:, w, :],
                                       start=(n == 0), stop=(n == 2))
                    mm.then_inc(ct_mm, 1)
                u = k + 2
                if within(u, NU):
                    wait(pe, normed, u + 1, 16, it)
                    wait(pe, pt_lo, u, 16, it)
                    for h in range(4):
                        mm = pe.transpose(t_bank[:, h * S:(h + 1) * S], prob[:, u % 4, h, :], ident_sb)
                    mm.then_inc(pt_mm, 1)
                u = k + 4
                if within(u, NU):
                    g, b, hg = u // 8, u // 4, u % 4
                    wait(pe, exped, u - 1, 16, it)
                    wait(pe, pr_lo, 8 * g + 2 * hg + 2, 16, it)
                    for pr in range(2):
                        mp = 2 * hg + pr
                        for n, (a, w) in enumerate(PASSES):
                            mm = pe.matmul(score_bank[u % 2][:, pr * 256:(pr + 1) * 256],
                                           lhsT=qT[g % 2][:, a, mp, (b % 2) * S:(b % 2 + 1) * S],
                                           rhs=kblk[g % 2][:, w, mp, b % 2, :], start=(n == 0), stop=(n == 2))
                    mm.then_inc(scored, 1)
                q = k + 12
                if within(q, 8 * NG):
                    g, j = q // 8, q % 8
                    wait(pe, pr_lo, q if q >= 8 else q - 1, 16, it)
                    if q in (0, 1):
                        pe.wait_ge(b_lo, 4 + 4 * q)
                    if q == 1:
                        pe.wait_ge(kr_lo, 1)
                    if j == 0:
                        wait(pe, ln_lo["l1"], 2 * (g + 1), 4, it)
                    if j == 1:
                        wait(pe, ropeT_step, 5 * (g + 1), 10, it)
                    for half in range(2):
                        mp = 2 * (j // 2) + half
                        cols = slice(mp * P, (mp + 1) * P)
                        o = piece_bank(q)[:, half * 256:(half + 1) * 256]
                        if j % 2 == 0:
                            for n in range(3 * KT):
                                t, (a, w) = n // 3, PASSES[n % 3]
                                mm = pe.matmul(o, lhsT=B_w[:, a, t, cols], rhs=xT1[g % 2][:, w, t, :],
                                               start=(n == 0), stop=(n == 3 * KT - 1))
                        else:
                            for n, (a, w) in enumerate(PASSES):
                                mm = pe.matmul(o, lhsT=Kr_w[:, a, cols], rhs=kvT[g % 2][:, w, :],
                                               start=(n == 0), stop=(n == 2))
                    mm.then_inc(pr_mm, 1)
                if -12 <= k < -4:
                    fuse_m(2 * (k + 12))
                    fuse_m(2 * (k + 12) + 1)
                misc(k, it)

            def misc_free(t1, b, bl, it):
                for s, c, top in ((ln_lo["l1"], t1, NB), (ln_up["l2"], b, NB), (lg_up, bl, NB)):
                    wait(pe, s, min(c, top) if it is None else c, 4, it)

            def misc(k, it):
                m = k % 8
                c = k // 8
                if m in (2, 3):
                    t1 = 2 * (c + 2) + m - 2
                    if within(t1, NB):
                        wait(pe, xn1_ready, t1 + 1, 4, it)
                        misc_free(t1, 2 * (c - 1), 2 * (c - 1), it)
                        ln_transposes(xn1[:, t1 % 2, :], ln_mm["l1"])
                if m in (4, 5):
                    b = 2 * (c - 1) + m - 4
                    if within(b, NB):
                        wait(pe, xn2_ready, b + 1, 4, it)
                        misc_free(2 * (c + 3), b, 2 * (c - 1), it)
                        ln_transposes(xn2[:, b % 2, :], ln_mm["l2"])
                if m in (6, 7):
                    b = 2 * (c - 1) + m - 6
                    if within(b, NB):
                        wait(pe, ln_up["l2"], b + 1, 4, it)
                        misc_free(2 * (c + 3), 2 * c, b, it)
                        for t in range(KT):
                            mm = pe.matmul(m_bank[:, 0:E], lhsT=xT32[:, b % 2, t * P:(t + 1) * P],
                                           rhs=router_sb[:, t * E:(t + 1) * E], start=(t == 0), stop=(t == KT - 1))
                        mm.then_inc(lg_mm, 1)

            def ln_transposes(rows, done):
                for t in range(KT):
                    mm = pe.transpose(m_bank[:, t * P:(t + 1) * P], rows[:, t * P:(t + 1) * P], ident_sb)
                mm.then_inc(done, 1)

            def fuse_m(h):
                pe.wait_ge(mf_lo, h + 1)
                if h < 2:
                    pe.wait_ge(b_lo, 5 + h)
                else:
                    pe.wait_ge(m_lo, h - 1)
                for n, (a, w) in enumerate(PASSES):
                    mm = pe.matmul(o_bank[h % 2][:, :], lhsT=mf_w[:, h % 4, a, D:], rhs=mf_w[:, h % 4, w, 0:D],
                                   start=(n == 0), stop=(n == 2))
                mm.then_inc(m_mm, 1)

            for half in range(2):
                for h in range(8):
                    if h % 4 == 0:
                        pe.wait_ge(wa_in[2 * half + h // 4], 32)
                    for t in range(3):
                        mm = pe.matmul(ab_bank[half][:, h * R:(h + 1) * R], lhsT=wqk_sb[:, t, 8 * half + h, :],
                                       rhs=wqr_sb[:, t, 8 * half + h, :], start=(t == 0), stop=(t == 2))
                mm.then_inc(a_mm, 1)
            pe.wait_ge(table_in, 32)
            for k in range(FIRST_STEP, -12):
                step(k, None)
            for n in range(8):
                half, t = n // KT, n % KT
                if n in (0, 3):
                    pe.wait_ge(a_lo, 1 + n // 3)
                if t == 0:
                    for odd in range(2):
                        pe.wait_ge(wq_lo[odd], 4 * (half + 1))
                if n >= 4:
                    pe.wait_ge(b_lo, n - 3)
                for h in range(8):
                    for i, (a, w) in enumerate(PASSES):
                        mm = pe.matmul(ab_bank[(n + 2) % 4][:, h * R:(h + 1) * R],
                                       lhsT=Wq_w[half][:, a, h, t * P:(t + 1) * P], rhs=A_w[:, w, 8 * half + h, :],
                                       start=(i == 0), stop=(i == 2))
                mm.then_inc(b_mm, 1)
            pe.wait_ge(const_in, 64)
            def gate_up(v, it, parts=(0, 1)):
                g, m = v // JT, v % JT
                wait(pe, h_mul, v - 1, 22, it)
                if m == 0:
                    wait(pe, xs_in[g % 2], 16 * (g // 2 + 1), 16, it)
                if g == 0:
                    pe.wait_ge(wsh_lo, 2 * (m + 1))
                for c in parts:
                    dst = (gate_bank, up_bank)[c][v % 2]
                    for n in range(3 * KT):
                        t, (a, w) = n // 3, PASSES[n % 3]
                        col = t * 2 * P + c * P
                        mm = pe.matmul(dst[:, :].rearrange("p (b n) -> p b n", b=4), lhsT=wsh[m][:, a, col:col + P],
                                       rhs=xs[g % 2][:, :, w * D + t * P:w * D + (t + 1) * P],
                                       start=(n == 0), stop=(n == 3 * KT - 1))
                if parts[-1] == 1:
                    mm.then_inc(gu_mm, 1)

            def down(v, it):
                g, m = v // JT, v % JT
                wait(pe, h_lo, v + 1, 22, it)
                if m == 0:
                    wait(pe, y_done, 4 * g, 8, it)
                for t in range(4):
                    for n, (a, w) in enumerate(PASSES):
                        mm = pe.matmul(acc_bank[t][:, :], lhsT=hsh[v % 2][:, a, t * P:(t + 1) * P],
                                       rhs=wsh[m][:, w, KT * 2 * P:], start=(m == 0 and n == 0),
                                       stop=(m == JT - 1 and n == 2))
                    if v == 8 * JT - 1:
                        mm.then_inc(acc_mm, 1)
                if m == JT - 1 and v < 8 * JT - 1:
                    mm.then_inc(acc_mm, 1)

            run_steps(pe, step, NU - 1)
            gate_up(0, None)
            for k in range(NU, LAST_STEP - 1):
                step(k, None)
            pe.wait_ge(x1_done, NB)
            down(0, None)
            for k in range(LAST_STEP - 1, LAST_STEP + 1):
                step(k, None)

            pe.wait_ge(x1_done, NB)
            pe.wait_ge(lg_up, NB)
            for v in range(22):
                if v == 4:
                    pe.wait_ge(masked, 1)
                    pe.wait_ge(h_mul, 3)
                    pe.matmul(gate_bank[0][:, 0:N8], lhsT=route_sb[:, 0:P], rhs=mask32, start=True, stop=True)
                    pe.matmul(gate_bank[0][:, N8:2 * N8], lhsT=route_sb[:, P:2 * P], rhs=mask32,
                              start=True, stop=True).then_inc(ranked, 1)
                    down(3, None)
                    pe.wait_ge(rank_up, 1)
                if v > 0:
                    gate_up(v, None)
                if v not in (0, 1, 4):
                    down(v - 1, None)
            down(21, None)
            gate_up(22, None, (0,))
            pe.wait_ge(y_done, 8)

            def expert_step(k, it):
                if within(k, NQ):
                    expert_gate_up(k, 0, it)
                if within(k + 1, NQ):
                    q = k + 1
                    wait(pe, xg_in[q % 2], 32 * (q // 2 + 1), 160, it)
                    wait(pe, xt_lo, 2 * q, 20, it)
                    for t in range(KT):
                        for b in range(2):
                            mm = pe.transpose(xt_bank[t // 2][:, (t % 2) * 256 + b * P:(t % 2) * 256 + (b + 1) * P],
                                              xg[q % 2][:, b, t * P:(t + 1) * P], ident_sb)
                    mm.then_inc(xt_mm, 1)
                if within(k, NQ):
                    expert_gate_up(k, 1, it)
                if within(k - 1, NQ):
                    expert_down(k - 1, 0, it)
                if within(k, NQ):
                    expert_gate_up(k, 2, it)
                if within(k - 1, NQ):
                    expert_down(k - 1, 1, it)

            def expert_gate_up(q, j, it):
                e = q // 5
                if j == 0:
                    wait(pe, xt_lo, 2 * (q + 1), 20, it)
                    if q % 5 == 0:
                        wait(pe, wx_lo, 4 * (e + 1), 8, it)
                n1 = 3 * q + j
                wait(pe, xmul, n1 - 1, 30, it)
                for c in range(2):
                    for n in range(3 * KT):
                        t, (a, w) = n // 3, PASSES[n % 3]
                        col = t * 2 * I + c * I + j * P
                        mm = pe.matmul(gu_bank[n1 % 2][0:IW[j], c * 256:(c + 1) * 256],
                                       lhsT=wx[e % 2][:, a, col:col + IW[j]], rhs=xgT[q % 2][:, w, t, :],
                                       start=(n == 0), stop=(n == 3 * KT - 1))
                mm.then_inc(xgu_mm, 1)

            def expert_down(q, b, it):
                e = q // 5
                n1 = 2 * q + b
                if b == 0:
                    wait(pe, xhl, 3 * (q + 1), 30, it)
                wait(pe, xo_up, n1 - 1, 20, it)
                for j in range(IT):
                    for n, (a, w) in enumerate(PASSES):
                        col = KT * 2 * I + j * D
                        mm = pe.matmul(xd_bank[b][:, :], lhsT=hx[q % 2][0:IW[j], a, j, b * P:(b + 1) * P],
                                       rhs=wx[e % 2][0:IW[j], w, col:col + D], start=(j == 0 and n == 0),
                                       stop=(j == IT - 1 and n == 2))
                mm.then_inc(xd_mm, 1)

            expert_step(-1, None)
            gate_up(22, None, (1,))
            pe.wait_ge(h_mul, 23)
            run_experts(pe, expert_step, 0)
            pe.wait_ge(xo_up, 2 * NQ)

            def shared_step(v, it):
                if 22 < v < 88:
                    gate_up(v, it)
                if v > 22:
                    down(v - 1, it)

            run_shared(pe, shared_step)

        @block.scalar
        def _(act):
            def step(k, it):
                m = k % 8
                u = k + 1
                if within(u, NU):
                    wait(act, ct_mm, u + 1, 16, it)
                    act.copy(cT[:, HI].rearrange("p h n -> p (h n)"), c_bank[:, :]).then_inc(ct_hi, 1)
                u = k + 2
                if within(u, NU):
                    wait(act, pt_mm, u + 1, 16, it)
                    act.copy(pT[:, HI, :], t_bank[:, :]).then_inc(pt_hi, 1)
                if k % 2 == 1:
                    upper_piece(k + 12, it)
                u = k + 4
                if within(u, NU):
                    wait(act, maxed, u + 1, 16, it)
                    for h in range(4):
                        mm = act.activation(prob[:, u % 4, h, :], score_bank[u % 2][:, h * S:(h + 1) * S], ACT.Exp,
                                            bias=neg_max[:, u % 4, h:h + 1], accum_out=den[:, u % 4, h:h + 1])
                    mm.then_inc(exped, 1)
                if k % 2 == 0:
                    upper_piece(k + 12, it)
                if -12 <= k < -4:
                    for h in (2 * (k + 12), 2 * (k + 12) + 1):
                        act.wait_ge(m_mm, h + 1)
                        act.copy(M_w[:, HI, h, :], o_bank[h % 2][:, :]).then_inc(m_hi, 1)
                    for h in (2 * (k + 12) + 4, 2 * (k + 12) + 5):
                        if h < H:
                            upper_mf(h)
                c = k // 8
                if m in (2, 3):
                    t1 = 2 * (c + 2) + m - 2
                    if within(t1, NB):
                        g = t1 // 2
                        wait(act, ln_mm["l1"], t1 + 1, 4, it)
                        act.copy(xT1[g % 2][:, HI, :, (t1 % 2) * S:(t1 % 2 + 1) * S],
                                 m_bank[:, :].rearrange("p (t n) -> p t n", t=KT)).then_inc(ln_up["l1"], 1)
                if m in (4, 5):
                    b = 2 * (c - 1) + m - 4
                    if within(b, NB):
                        wait(act, ln_mm["l2"], b + 1, 4, it)
                        wait(act, ln_lo["l2"], b - 1, 4, it)
                        wait(act, xT2_out[b % 2], 16 * (b // 2), 32, it)
                        act.copy(xT32[:, b % 2, :], m_bank[:, :])
                        act.copy(xT2[b % 2][:, HI].rearrange("p t n -> p (t n)"),
                                 m_bank[:, :]).then_inc(ln_up["l2"], 1)
                if m in (6, 7):
                    b = 2 * (c - 1) + m - 6
                    if within(b, NB):
                        wait(act, lg_mm, b + 1, 4, it)
                        act.copy(logits[:, b, :] if it is None else logits[:, bass.ds(at(b, 4, it), 1), :],
                                 m_bank[:, 0:E] if it is None else
                                 m_bank[:, 0:E].rearrange("p (o e) -> p o e", o=1)).then_inc(lg_up, 1)
                if it is None and within(k - FFN_FIRST, 12):
                    split_wsh(k - FFN_FIRST)

            def upper_mf(h):
                act.wait_ge(wo_in[h % 4], 32 * (h // 4 + 1))
                wait(act, m_mm, h - 3, 0, None)
                act.copy(mf_w[:, h % 4, HI, :], mf_ring[:, h % 4, :]).then_inc(mf_hi, 1)

            def upper_piece(q, it):
                if within(q, 8 * NG):
                    wait(act, pr_mm, q + 1, 16, it)
                    g, j = q // 8, q % 8
                    jp = slice(2 * (j // 2), 2 * (j // 2) + 2)
                    src = piece_bank(q)
                    if j % 2 == 0:
                        act.copy(qT[g % 2][:, HI, jp, :],
                                 src[:, :].rearrange("p (m n) -> p m n", m=2)).then_inc(pr_hi, 1)
                    else:
                        if q in (1, 9):
                            act.wait_ge(kblk_zero, 1 + q // 9)
                        for s in range(2):
                            i = act.copy(kblk[g % 2][s * R:(s + 1) * R, HI, jp, :, s * S:(s + 1) * S],
                                         src[s * R:(s + 1) * R, :].rearrange("p (m b n) -> p m b n", m=2, b=2))
                        i.then_inc(pr_hi, 1)

            def split_wsh(n):
                act.wait_ge(wsh_in[n % 3], 16 * (n // 3 + 1))
                act.copy(wsh[n // 2][:, HI, (n % 2) * PIECE:(n % 2 + 1) * PIECE], wsh_raw[:, n % 3, :])\
                    .then_inc(wsh_hi, 1)

            def split_wx(n, it):
                e, r = n // 4, n % 4
                wait(act, wx_in[n % 2], 16 * (n // 2 + 1), 64, it)
                if r == 0:
                    wait(act, xd_mm, 10 * (e - 1), 20, it)
                act.copy(wx[e % 2][:, HI, r * XPIECE:(r + 1) * XPIECE], wx_raw[:, n % 2, :]).then_inc(wx_hi, 1)

            def upper_a(half):
                act.wait_ge(a_mm, half + 1)
                act.copy(A_w[:, HI, 8 * half:8 * half + 8, :].rearrange("p h r -> p (h r)"),
                         ab_bank[half][:, :]).then_inc(a_hi, 1)

            def upper_wq(h):
                if h % 4 == 0:
                    act.wait_ge(wq_in[h // 4], 16)
                act.copy(Wq_w[h // 8][:, HI, h % 8, :], Wq_sb[:, h, :]).then_inc(wq_hi, 1)

            def upper_b(n):
                act.wait_ge(b_mm, n + 1)
                act.copy(B_w[:, HI, n % KT, (n // KT) * 512:(n // KT + 1) * 512],
                         ab_bank[(n + 2) % 4][:, :]).then_inc(b_hi, 1)

            upper_a(0)
            for h in range(8):
                upper_wq(h)
            upper_a(1)
            for k in range(FIRST_STEP, -12):
                step(k, None)
            for n in range(4):
                upper_wq(8 + 2 * n)
                upper_wq(9 + 2 * n)
                upper_b(n)
            for h in range(4):
                upper_mf(h)
            act.wait_ge(kr_in, 16)
            act.copy(Kr_w[:, HI, :], kr_stage).then_inc(kr_hi, 1)
            act.wait_ge(const_in, 64)
            act.activation(tanh_sb, gate_sb, ACT.Tanh).then_inc(tanh_done, 1)
            for n in range(4, 8):
                upper_b(n)

            def silu_step(v, it):
                wait(act, gu_mm, v + 1, 22, it)
                act.activation(silu[v % 2], gate_bank[v % 2][:, :], ACT.Silu).then_inc(silu_done, 1)

            run_steps(act, step, NU + 3)
            silu_step(0, None)
            for k in range(NU + 4, LAST_STEP + 1):
                step(k, None)

            silu_step(1, None)
            attention_over(act)
            for v in range(1, 22):
                if v == 4:
                    act.wait_ge(ranked, 1)
                    act.copy(rt_rank, gate_bank[0][:, 0:N8])
                    act.copy(rt_count, gate_bank[0][:, N8:2 * N8]).then_inc(rank_up, 1)
                if v > 1:
                    silu_step(v, None)
                if v < 6:
                    split_wsh(10 + 2 * v)
                    split_wsh(11 + 2 * v)
                if v == 3:
                    act.wait_ge(gap_done, 1)
                    act.activation(rt_exp, rt_gap, ACT.Exp).then_inc(exp_done, 1)
                if 16 <= v < 20:
                    split_wx(v - 16, None)

            def expert_step(k, it):
                e = (k + 4) // 5
                if 1 <= e < E and (k + 4) % 5 < 4:
                    split_wx(4 * e + (k + 4) % 5, it)
                for j in range(IT):
                    if within(k, NQ):
                        n1 = 3 * k + j
                        wait(act, xgu_mm, n1 + 1, 30, it)
                        act.activation(silu[n1 % 2][0:IW[j], 0:256], gu_bank[n1 % 2][0:IW[j], 0:256],
                                       ACT.Silu).then_inc(xsilu, 1)
                    if j == 0 and within(k + 1, NQ):
                        q = k + 1
                        wait(act, xt_mm, q + 1, 10, it)
                        for i in range(2):
                            act.copy(xgT[q % 2][:, HI, 2 * i:2 * i + 2, :].rearrange("p t n -> p (t n)"),
                                     xt_bank[i][:, :]).then_inc(xt_hi, 1)
                    if j == 1 and within(k - 1, NQ):
                        row_out(2 * (k - 1), it)
                if within(k - 1, NQ):
                    row_out(2 * (k - 1) + 1, it)
            def row_out(n1, it):
                wait(act, xd_mm, n1 + 1, 20, it)
                wait(act, xo_out[n1 % 4], 16 * (n1 // 4), 80, it)
                act.copy(xo[:, n1 % 4, :], xd_bank[n1 % 2][:, :]).then_inc(xo_up, 1)

            expert_step(-1, None)
            silu_step(22, None)
            run_experts(act, expert_step, 0)

            def shared_step(v, it):
                if 22 < v < 88:
                    silu_step(v, it)

            run_shared(act, shared_step)

        @block.vector
        def _(dve):
            def lower(dst, src, hi):
                return dve.tensor_tensor(dst, src, hi, ALU.subtract)

            def step(k, it):
                m = k % 8
                c = k // 8
                g2, g1 = c - 1, c + 2

                def links(*which):
                    if m in (0, 1) and (within(g2, NG) or within(g1, NG)):
                        for i in which:
                            rsqrt_link(i, g2, g1, it)

                u = k + 3
                if within(u, NU):
                    wait(dve, exped, u + 1, 16, it)
                    dve.reciprocal(rden[:, u % 4, :], den[:, u % 4, :]).then_inc(inverted, 1)
                links(*((1, 2) if m == 0 else (10, 11)))
                if k % 4 == 3 and within(k // 4, NB):
                    b = k // 4
                    wait(dve, o_mm, b + 1, 4, it)
                    wait(dve, xres_in[b % 2], 16 * (b // 2 + 1), 32, it)
                    if b == 0:
                        dve.wait_ge(tanh_done, 1)
                    dve.scalar_tensor_tensor(out=x1[:, b % 2, :], in0=o_bank[b % 2][:, :], scalar=tanh_sb[:, 0:1],
                                             in1=x1[:, b % 2, :], op0=ALU.mult, op1=ALU.add).then_inc(x1_done, 1)
                u = k + 1
                if within(u, NU):
                    wait(dve, ct_hi, u + 1, 16, it)
                    lower(cT[:, LO].rearrange("p h n -> p (h n)"), c_bank[:, :],
                          cT[:, HI].rearrange("p h n -> p (h n)")).then_inc(ct_lo, 1)
                links(*((3, 4) if m == 0 else (12, 13)))
                u = k + 2
                if within(u, NU):
                    wait(dve, pt_hi, u + 1, 16, it)
                    lower(pT[:, LO, :], t_bank[:, :], pT[:, HI, :]).then_inc(pt_lo, 1)
                links(*((5,) if m == 0 else (14,)))
                u = k + 4
                if within(u, NU):
                    wait(dve, scored, u + 1, 16, it)
                    dve.tensor_reduce(neg_max[:, u % 4, :], score_bank[u % 2][:, :].rearrange("p (h n) -> p h n", h=4),
                                      AX.X, ALU.max, negate=True).then_inc(maxed, 1)
                links(*((6, 7) if m == 0 else (15, 16)))
                q = k + 12
                if within(q, 8 * NG):
                    wait(dve, pr_hi, q + 1, 16, it)
                    g, j = q // 8, q % 8
                    jp = slice(2 * (j // 2), 2 * (j // 2) + 2)
                    src = piece_bank(q)
                    if j % 2 == 0:
                        lower(qT[g % 2][:, LO, jp, :], src[:, :].rearrange("p (m n) -> p m n", m=2),
                              qT[g % 2][:, HI, jp, :]).then_inc(pr_lo, 1)
                    else:
                        for s in range(2):
                            rows, cols = slice(s * R, (s + 1) * R), slice(s * S, (s + 1) * S)
                            i = lower(kblk[g % 2][rows, LO, jp, :, cols],
                                      src[rows, :].rearrange("p (m b n) -> p m b n", m=2, b=2),
                                      kblk[g % 2][rows, HI, jp, :, cols])
                        i.then_inc(pr_lo, 1)
                if m in (2, 3):
                    t1 = 2 * (c + 2) + m - 2
                    if within(t1, NB):
                        wait(dve, ln_up["l1"], t1 + 1, 4, it)
                        dst = xT1[(t1 // 2) % 2][:, :, :, (t1 % 2) * S:(t1 % 2 + 1) * S]
                        lower(dst[:, LO], m_bank[:, :].rearrange("p (t n) -> p t n", t=KT),
                              dst[:, HI]).then_inc(ln_lo["l1"], 1)
                links(*((8, 9) if m == 0 else (17,)))
                if m == 1:
                    norms(g2, g1, it)
                if -12 <= k < -4:
                    for h in (2 * (k + 12), 2 * (k + 12) + 1):
                        dve.wait_ge(m_hi, h + 1)
                        lower(M_w[:, LO, h, :], o_bank[h % 2][:, :], M_w[:, HI, h, :]).then_inc(m_lo, 1)
                if k % 4 == 3 and within(k // 4, NB):
                    b = k // 4
                    wait(dve, x1_done, b + 1, 4, it)
                    dve.bn_stats(stats[:, b % 2, :], x1[:, b % 2, :]).then_inc(stat2, 1)
                if m == 6 and within(c + 3, NG):
                    g = c + 3
                    wait(dve, xln_in, 16 * (g + 1), 32, it)
                    for s in range(2):
                        dve.bn_stats(stats[:, 2 + s, :], x_ln[:, s, :]).then_inc(stat1, 1)

            def rsqrt_link(i, g2, g1, it):
                has2, has1 = within(g2, NG), within(g1, NG)
                cols = slice(0 if has2 else 2, 4 if has1 else 2)
                v, y, n = var_eps[:, cols], rstd[:, cols], newton[:, cols]
                m_e, m_o, q_e, q_o = (stats[:, cols, f] for f in (1, 4, 2, 5))
                mu, dif = mean[:, cols], mean_dif[:, cols]
                if i == 1:
                    if has2:
                        wait(dve, stat2, 2 * g2 + 2, 4, it)
                    if has1:
                        wait(dve, stat1, 2 * g1 + 2, 4, it)
                    dve.tensor_tensor(mu, m_e, m_o, ALU.add)
                    dve.tensor_tensor(dif, m_e, m_o, ALU.subtract)
                    dve.tensor_tensor(v, q_e, q_o, ALU.add).then_inc(rsqrt_step, 1)
                    return
                wait(dve, rsqrt_step, RSQRT_OPS * g1 + i - 1, 2 * RSQRT_OPS, it)
                if i == 2:
                    dve.tensor_scalar(mu, mu, 0.5, None, ALU.mult)
                    dve.tensor_tensor(dif, dif, dif, ALU.mult)
                    ins = dve.tensor_scalar(v, v, 1.0 / D, EPS, ALU.mult, ALU.add)
                elif i == 3:
                    ins = dve.scalar_tensor_tensor(out=v, in0=dif, scalar=0.25, in1=v, op0=ALU.mult, op1=ALU.add)
                elif i == 4:
                    ins = dve.tensor_scalar(shifted[:, cols].bitcast(I32), v.bitcast(I32), 1, None,
                                            ALU.arith_shift_right)
                elif i == 5:
                    ins = dve.tensor_scalar(y.bitcast(I32), shifted[:, cols].bitcast(I32), -1.0, RSQRT_SEED,
                                            ALU.mult, ALU.add)
                elif i % 4 == 2:
                    ins = dve.tensor_tensor(n, v, y, ALU.mult)
                elif i % 4 == 3:
                    ins = dve.tensor_tensor(n, n, y, ALU.mult)
                elif i % 4 == 0:
                    ins = dve.tensor_scalar(n, n, -0.5, 1.5, ALU.mult, ALU.add)
                else:
                    ins = dve.tensor_tensor(y, y, n, ALU.mult)
                ins.then_inc(rsqrt_step, 1)

            def norms(g2, g1, it):
                if within(g2, NG) or within(g1, NG):
                    wait(dve, rsqrt_step, RSQRT_OPS * (g1 + 1), 2 * RSQRT_OPS, it)
                if within(g1, NG):
                    for s in range(2):
                        wait(dve, ln_mm["l1"], 2 * g1 + s - 1, 4, it)
                        dve.tensor_scalar(xn1[:, s, :], x_ln[:, s, :], mean[:, 2 + s:3 + s],
                                          rstd[:, 2 + s:3 + s], ALU.subtract, ALU.mult).then_inc(xn1_ready, 1)
                if within(g2, NG):
                    for s in range(2):
                        b = 2 * g2 + s
                        wait(dve, xn2_out[s], 16 * g2, 32, it)
                        wait(dve, ln_mm["l2"], b - 1, 4, it)
                        dve.tensor_scalar(xn2[:, s, :], x1[:, s, :], mean[:, s:s + 1], rstd[:, s:s + 1],
                                          ALU.subtract, ALU.mult).then_inc(xn2_ready, 1)

            def lower_a(half):
                dve.wait_ge(a_hi, half + 1)
                lower(A_w[:, LO, 8 * half:8 * half + 8, :].rearrange("p h r -> p (h r)"), ab_bank[half][:, :],
                      A_w[:, HI, 8 * half:8 * half + 8, :].rearrange("p h r -> p (h r)")).then_inc(a_lo, 1)

            def lower_wq(h):
                dve.wait_ge(wq_hi, h + 1)
                lower(Wq_w[h // 8][:, LO, h % 8, :], Wq_sb[:, h, :], Wq_w[h // 8][:, HI, h % 8, :])\
                    .then_inc(wq_lo[0], 1)

            def lower_b(n):
                dve.wait_ge(b_hi, n + 1)
                cols = slice((n // KT) * 512, (n // KT + 1) * 512)
                lower(B_w[:, LO, n % KT, cols], ab_bank[(n + 2) % 4][:, :], B_w[:, HI, n % KT, cols]).then_inc(b_lo, 1)

            for k in range(FIRST_STEP, -14):
                step(k, None)
            lower_a(0)
            for h in range(0, 8, 2):
                lower_wq(h)
            lower_a(1)
            for k in range(-14, -12):
                step(k, None)
            for n in range(4):
                lower_wq(8 + 2 * n)
                lower_b(n)
            dve.wait_ge(kr_hi, 1)
            lower(Kr_w[:, LO, :], kr_stage, Kr_w[:, HI, :]).then_inc(kr_lo, 1)
            for n in range(4, 8):
                lower_b(n)
            run_steps(dve, step)

            def hidden(v, it):
                wait(dve, silu_done, v + 1, 22, it)
                dve.tensor_tensor(h32[v % 2], silu[v % 2], up_bank[v % 2][:, :], ALU.mult).then_inc(h_mul, 1)
                wait(dve, h_mul, v + 1, 22, it)
                dve.tensor_copy(hsh[v % 2][:, HI, :], h32[v % 2]).then_inc(h_hi, 1)
                wait(dve, h_hi, v + 1, 22, it)
                lower(hsh[v % 2][:, LO, :], h32[v % 2], hsh[v % 2][:, HI, :]).then_inc(h_lo, 1)

            def add_shared(g, it):
                if g < 7:
                    wait(dve, acc_mm, g + 1, 2, it)
                wait(dve, y_in, 16 * (g + 1 if it is None and g < 2 else g + 3), 32, it)
                for t in range(4):
                    if g == 7:
                        dve.wait_ge(comb_2, 28 + t + 1)
                        dve.wait_ge(acc_mm, 8 + t)
                    dve.scalar_tensor_tensor(out=y_sb[:, t, :], in0=acc_bank[t][:, :], scalar=tanh_sb[:, 1:2],
                                             in1=y_sb[:, t, :], op0=ALU.mult, op1=ALU.add).then_inc(y_done, 1)

            def add_experts(t, it):
                i = t % 4
                wait(dve, r_in, 128 * (t // 4 + 1), 256, it)
                if 8 <= t < 28:
                    wait(dve, y_done, t + 1, 8, it)
                elif i == 0:
                    wait(dve, y_in, 16 * (t // 4 + 3), 0, None)
                for c, done in enumerate((comb_1, comb_2)):
                    dve.scalar_tensor_tensor(out=y_sb[:, i, :], in0=r_sb[:, 2 * i + c, :],
                                             scalar=weight_now[:, 2 * i + c:2 * i + c + 1], in1=y_sb[:, i, :],
                                             op0=ALU.mult, op1=ALU.add).then_inc(done, 1)
                    if c == 0:
                        wait(dve, comb_1, t + 1, 8, it)

            links = [0]

            def link(ins):
                links[0] += 1
                ins.then_inc(route_step, 1)
                dve.wait_ge(route_step, links[0])

            def tiles(v):
                return v.unsqueeze(2).broadcast_to([P, NB, E])

            def per(v):
                return v.rearrange("p (b e) -> p b e", e=E)

            def choose():
                ramp = route_sb[:, 2 * P:2 * P + E].unsqueeze(1).broadcast_to([P, NB, E])
                source = logits
                for c in range(2):
                    link(dve.tensor_reduce(rt_top[:, c, :], source, AX.X, ALU.max))
                    link(dve.tensor_tensor(per(rt_a), source, tiles(rt_top[:, c, :]), ALU.is_equal))
                    link(dve.tensor_tensor(per(rt_a), per(rt_a), ramp, ALU.mult))
                    link(dve.tensor_reduce(rt_rev[:, c, :], per(rt_a), AX.X, ALU.max))
                    link(dve.tensor_tensor(per(rt_hot[:, c, :]), ramp, tiles(rt_rev[:, c, :]), ALU.is_equal))
                    if c == 0:
                        link(dve.scalar_tensor_tensor(out=per(rt_b), in0=per(rt_hot[:, 0, :]), scalar=-3.0e38,
                                                      in1=logits, op0=ALU.mult, op1=ALU.add))
                        source = per(rt_b)
                dve.tensor_tensor(mask32, rt_hot[:, 0, :], rt_hot[:, 1, :], ALU.add).then_inc(masked, 1)
                dve.tensor_tensor(rt_gap, rt_top[:, 1, :], rt_top[:, 0, :], ALU.subtract).then_inc(gap_done, 1)
                dve.memset(rt_sum[:, 0, 0:P], 0.0)
                link(dve.memset(rt_sum[:, 1, 0:P], 0.0))

            def place():
                dve.wait_ge(rank_up, 1)
                link(dve.tensor_copy(rt_sum[:, 0, P:], rt_count))
                for i in range(5):
                    a, b = rt_sum[:, i % 2, :], rt_sum[:, (i + 1) % 2, :]
                    shift = E << i
                    link(dve.tensor_tensor(b[:, P:], a[:, P:], a[:, P - shift:P - shift + N8], ALU.add))
                link(dve.tensor_tensor(rt_a, rt_sum[:, 1, P:], rt_count, ALU.subtract))
                link(dve.tensor_tensor(rt_b, rt_a, rt_rank, ALU.add))
                dve.wait_ge(exp_done, 1)
                link(dve.tensor_scalar(rt_pos, rt_exp, 1.0, None, ALU.add))
                link(dve.reciprocal(rt_share[:, 0, :], rt_pos))
                link(dve.tensor_tensor(rt_share[:, 1, :], rt_share[:, 0, :], rt_exp, ALU.mult))

            def slots(c):
                link(dve.tensor_tensor(rt_a, rt_hot[:, c, :], rt_b, ALU.mult))
                link(dve.tensor_reduce(rt_pos, per(rt_a), AX.X, ALU.add))
                link(dve.tensor_scalar(rt_valid, rt_pos, float(CAP), None, ALU.is_lt))
                link(dve.tensor_scalar(rt_c, rt_rev[:, c, :], -float(CAP), float(E * CAP), ALU.mult, ALU.add))
                link(dve.tensor_tensor(rt_pos, rt_pos, rt_c, ALU.add))
                link(dve.tensor_tensor(rt_c, rt_pos, rt_valid, ALU.mult))
                link(dve.tensor_copy(slot_of[:, :, c], rt_c))
                link(dve.tensor_scalar(rt_c, rt_valid, -2.0 * E * CAP, 2.0 * E * CAP, ALU.mult, ALU.add))
                link(dve.tensor_tensor(rt_c, rt_c, rt_pos, ALU.add))
                link(dve.tensor_copy(scatter_to[:, :, c], rt_c))
                link(dve.tensor_scalar(rt_c, rt_share[:, c, :], tanh_sb[:, 1:2], None, ALU.mult))
                dve.tensor_tensor(weight_of[:, :, c], rt_c, rt_valid, ALU.mult).then_inc(routed, 1)
                dve.wait_ge(routed, c + 1)

            hidden(0, None)
            hidden(1, None)
            def lower_wsh(n):
                dve.wait_ge(wsh_hi, n + 1)
                cols = slice((n % 2) * PIECE, (n % 2 + 1) * PIECE)
                lower(wsh[n // 2][:, LO, cols], wsh_raw[:, n % 3, :], wsh[n // 2][:, HI, cols]).then_inc(wsh_lo, 1)

            attention_over(dve)
            lower_wsh(12)
            lower_wsh(13)
            choose()
            for v in range(2, 22):
                hidden(v, None)
                if v < 6:
                    lower_wsh(10 + 2 * v)
                    lower_wsh(11 + 2 * v)
                if v == 5:
                    place()
                if v == 6:
                    slots(0)
                if v == 7:
                    slots(1)
                if v == 11:
                    add_shared(0, None)
            add_shared(1, None)

            def expert_step(k, it):
                for j in range(IT):
                    if within(k, NQ):
                        n1 = 3 * k + j
                        rows = slice(0, IW[j])
                        wait(dve, xsilu, n1 + 1, 30, it)
                        dve.tensor_tensor(h32[n1 % 2][rows, 0:256], silu[n1 % 2][rows, 0:256],
                                          gu_bank[n1 % 2][rows, 256:512], ALU.mult).then_inc(xmul, 1)
                        wait(dve, xmul, n1 + 1, 30, it)
                        dve.tensor_copy(hx[k % 2][rows, HI, j, :], h32[n1 % 2][rows, 0:256]).then_inc(xhh, 1)
                        wait(dve, xhh, n1 + 1, 30, it)
                        lower(hx[k % 2][rows, LO, j, :], h32[n1 % 2][rows, 0:256],
                              hx[k % 2][rows, HI, j, :]).then_inc(xhl, 1)
                    if j == 0 and within(k + 1, NQ):
                        q = k + 1
                        for i in range(2):
                            wait(dve, xt_hi, 2 * q + i + 1, 20, it)
                            lower(xgT[q % 2][:, LO, 2 * i:2 * i + 2, :].rearrange("p t n -> p (t n)"),
                                  xt_bank[i][:, :],
                                  xgT[q % 2][:, HI, 2 * i:2 * i + 2, :].rearrange("p t n -> p (t n)"))\
                                .then_inc(xt_lo, 1)

            expert_step(-1, None)
            hidden(22, None)
            dve.wait_ge(h_lo, 23)
            run_experts(dve, expert_step, 0)

            def shared_step(v, it):
                g, m = v // JT, v % JT
                if 22 < v < 88:
                    hidden(v, it)
                if m == 0 and g > 2:
                    add_shared(g - 1, it)
                if v >= 84 and v < 88:
                    add_experts(28 + v - 84, None)
                if 24 <= v < 32:
                    add_experts(v - 24, None)
                if v >= 34 and 1 <= m <= 4:
                    add_experts(4 * (g - 1) + m - 1, it)

            run_shared(dve, shared_step)

        @block.gpsimd
        def _(pool):
            tab = table_sb.rearrange("p (i n) -> p i n", i=4)

            def both(t):
                return tab[:, t, :].unsqueeze(1).broadcast_to([P, 2, P])

            def step(k, it):
                m = k % 8
                c = k // 8
                if -12 <= k < -6:
                    lower_mf(2 * (k + 12) + 4)
                    lower_mf(2 * (k + 12) + 5)
                if k == -6:
                    pool.wait_ge(b_mm, 4)
                    pool.memset(k_region[:, 4096:8192], 0.0).then_inc(kblk_zero, 1)
                u = k + 3
                if within(u, NU):
                    wait(pool, inverted, u + 1, 16, it)
                    pool.tensor_tensor(prob[:, u % 4], prob[:, u % 4],
                                       rden[:, u % 4, :].unsqueeze(2).broadcast_to([P, 4, S]),
                                       ALU.mult).then_inc(normed, 1)
                if m in (4, 5):
                    b = 2 * (c - 1) + m - 4
                    if within(b, NB):
                        wait(pool, ln_up["l2"], b + 1, 4, it)
                        pool.tensor_tensor(xT2[b % 2][:, LO].rearrange("p t n -> p (t n)"), xT32[:, b % 2, :],
                                           xT2[b % 2][:, HI].rearrange("p t n -> p (t n)"),
                                           ALU.subtract).then_inc(ln_lo["l2"], 1)
                if m == 0 and within(c + 2, NG):
                    g = c + 2
                    raw = kvT_raw.rearrange("p r (b n) -> p r b n", b=2)
                    a, b = (r.rearrange("p (b n) -> p b n", b=2) for r in (rope_a, rope_b))
                    base = 5 * g

                    def link(ins, i):
                        ins.then_inc(ropeT_step, 1)
                        wait(pool, ropeT_step, base + i, 10, it)

                    wait(pool, kvt_in, 16 * (g + 1), 32, it)
                    wait(pool, pr_mm, 8 * (g - 1), 16, it)
                    wait(pool, ropeN_step, max(6 * (g - 3) + 6, 0), 12, it)
                    link(pool.tensor_tensor(a, raw[:, 0], both(0), ALU.mult), 1)
                    link(pool.tensor_tensor(b, raw[:, 1], both(1), ALU.mult), 2)
                    link(pool.tensor_tensor(kvT[g % 2][:, HI, :], rope_a, rope_b, ALU.add), 3)
                    link(pool.tensor_tensor(a, a, b, ALU.add), 4)
                    link(pool.tensor_tensor(kvT[g % 2][:, LO, :], rope_a, kvT[g % 2][:, HI, :], ALU.subtract), 5)
                if m == 4 and within((k + 4) // 8, NG):
                    g = (k + 4) // 8
                    a, b = (r.rearrange("p (b n) -> p b n", b=2) for r in (rope_a, rope_b))
                    base = 6 * g

                    def link(ins, i):
                        ins.then_inc(ropeN_step, 1)
                        wait(pool, ropeN_step, base + i, 12, it)

                    wait(pool, kvn_in, 16 * (g + 1), 32, it)
                    wait(pool, ct_mm, 8 * (g - 1), 16, it)
                    hf = P // 2
                    link(pool.tensor_tensor(a, kvN_raw, both(2), ALU.mult), 1)
                    link(pool.tensor_tensor(b[:, :, 0:hf], kvN_raw[:, :, hf:P],
                                            tab[:, 3, 0:hf].unsqueeze(1).broadcast_to([P, 2, hf]), ALU.mult), 2)
                    link(pool.tensor_tensor(b[:, :, hf:P], kvN_raw[:, :, 0:hf],
                                            tab[:, 3, hf:P].unsqueeze(1).broadcast_to([P, 2, hf]), ALU.mult), 3)
                    link(pool.tensor_tensor(kvN[g % 2][:, HI], a, b, ALU.add), 4)
                    link(pool.tensor_tensor(a, a, b, ALU.add), 5)
                    link(pool.tensor_tensor(kvN[g % 2][:, LO], a, kvN[g % 2][:, HI], ALU.subtract), 6)
                if it is None and within(k - FFN_FIRST, 12):
                    lower_wsh(k - FFN_FIRST)

            def lower_mf(h):
                pool.wait_ge(mf_hi, h + 1)
                pool.tensor_tensor(mf_w[:, h % 4, LO, :], mf_ring[:, h % 4, :], mf_w[:, h % 4, HI, :],
                                   ALU.subtract).then_inc(mf_lo, 1)

            def lower_wsh(n):
                pool.wait_ge(wsh_hi, n + 1)
                cols = slice((n % 2) * PIECE, (n % 2 + 1) * PIECE)
                pool.tensor_tensor(wsh[n // 2][:, LO, cols], wsh_raw[:, n % 3, :], wsh[n // 2][:, HI, cols],
                                   ALU.subtract).then_inc(wsh_lo, 1)

            pool.memset(zero_ids, 0).then_inc(zeroed, 1)
            pool.memset(one, 1.0).then_inc(zeroed, 1)
            pool.memset(k_region[:, 0:4096], 0.0).then_inc(kblk_zero, 1)
            pool.wait_ge(zeroed, 2)
            pool.wait_ge(table_in, 32)
            for k in range(FIRST_STEP, -12):
                step(k, None)
            for h in range(1, H, 2):
                pool.wait_ge(wq_hi, h + 1)
                pool.tensor_tensor(Wq_w[h // 8][:, LO, h % 8, :], Wq_sb[:, h, :], Wq_w[h // 8][:, HI, h % 8, :],
                                   ALU.subtract).then_inc(wq_lo[1], 1)
            for h in range(4):
                lower_mf(h)
            pool.wait_ge(const_in, 64)
            run_steps(pool, step)

            def wait_first(s, c, per, it, i):
                wait(pool, s, c, per, it)
                if it is not None:
                    pool.tensor_tensor(waited[:, i:i + 1], one, one, ALU.add)

            attention_over(pool)
            pool.wait_ge(routed, 2)
            pool.wait_ge(ids_zero, 16)
            for b in range(NB):
                for c in range(2):
                    pool.indirect_dma_start(
                        out=slot_token_d, out_offset=bass.IndirectOffsetOnAxis(ap=scatter_to[:, b, c:c + 1], axis=0),
                        in_=token_sb[:, b:b + 1], in_offset=None, bounds_check=E * CAP - 1,
                        oob_is_err=False).then_inc(scattered, 16)

            def lower_wx(n, it):
                e, cols = n // 4, slice((n % 4) * XPIECE, (n % 4 + 1) * XPIECE)
                wait(pool, wx_hi, n + 1, 8, it)
                pool.tensor_tensor(wx[e % 2][:, LO, cols], wx_raw[:, n % 2, :], wx[e % 2][:, HI, cols],
                                   ALU.subtract).then_inc(wx_lo, 1)

            for n in range(4):
                lower_wx(n, None)

            xn2_rows = xn2_d.rearrange("b s d -> (b s) d")

            def gather(q, it):
                e = q // 5
                if q % 5 == 0:
                    wait_first(ids_in[e % 2], 16 * (e // 2 + 1), 16, it, 10 + e % 2)
                wait_first(xt_mm, q - 1, 10, it, q % 10)
                for b in range(2):
                    i = 2 * (q % 5) + b
                    pool.indirect_dma_start(
                        out=xg[q % 2][:, b, :], out_offset=None, in_=xn2_rows,
                        in_offset=bass.IndirectOffsetOnAxis(ap=ids[:, e % 2, i:i + 1], axis=0))\
                        .then_inc(xg_in[q % 2], 16)

            def expert_step(k, it):
                if k == -1:
                    gather(0, None)
                e = (k + 4) // 5
                if 1 <= e < E and (k + 4) % 5 < 4:
                    lower_wx(4 * e + (k + 4) % 5, it)
                if within(k + 2, NQ):
                    gather(k + 2, it)

            run_experts(pool, expert_step)

            def gather_rows(s, it):
                wait_first(comb_2, 4 * s, 8, it, 12 + s % 2)
                cols = at(4 * s, 8, it)
                src = lambda v: (v[:, cols:cols + 4, :] if it is None else v[:, bass.ds(cols, 4), :])
                pool.tensor_copy(weight_now.rearrange("p (b c) -> p b c", c=2), src(weight_of))
                pool.tensor_copy(slot_now.rearrange("p (b c) -> p b c", c=2), src(slot_of)).then_inc(now_done, 1)
                wait_first(now_done, s + 1, 2, it, 14 + s % 2)
                for i in range(8):
                    pool.indirect_dma_start(out=r_sb[:, i, :], out_offset=None, in_=xrow_d,
                                            in_offset=bass.IndirectOffsetOnAxis(ap=slot_now[:, i:i + 1], axis=0))\
                        .then_inc(r_in, 16)

            def shared_step(v, it):
                g, m = v // JT, v % JT
                if v in (22, 28):
                    gather_rows(0 if v == 22 else 1, None)
                if v == 32:
                    gather_rows(2, None)
                if v >= 34 and m == 5 and g < 8:
                    gather_rows(g, it)

            pool.wait_ge(xd_mm, 2 * NQ)
            pool.wait_ge(xt_lo, 2 * NQ)
            for i in range(4):
                pool.wait_ge(xo_out[i], 16 * NQ // 2)
            run_shared(pool, shared_step)


def kernel(**inputs):
    import numpy as np
    import concourse.bacc as bacc
    from concourse.bass_utils import run_bass_kernel_spmd as run

    nc = bacc.Bacc("TRN2", target_bir_lowering=False, num_devices=1)
    f = {k: np.asarray(v) for k, v in inputs.items()}
    ctxt = f["ctx_512"].reshape(NG, 2, S, P)
    kv_t = ctxt.transpose(0, 3, 1, 2)
    kv_t = np.stack([kv_t, np.concatenate([kv_t[:, P // 2:], kv_t[:, :P // 2]], axis=1)], axis=2)
    inv = (np.float32(1.0) / np.float32(10000.0) ** (np.arange(0, P, 2, dtype=np.float32) / np.float32(P)))
    freq = np.arange(S, dtype=np.float32)[:, None] * inv[None, :].astype(np.float32)
    sin = np.repeat(np.sin(freq), 2, axis=-1).astype(np.float32)
    cos = np.repeat(np.cos(freq), 2, axis=-1).astype(np.float32)
    sin[:, :P // 2] *= -1
    gu = f["L0_ffn_shared_w_up_gate"].reshape(KT, P, 2, JT, P).transpose(3, 1, 0, 2, 4).reshape(JT, P, KT * 2 * P)
    w_shared = np.concatenate([gu, f["L0_ffn_shared_w_down"].reshape(JT, P, D)], axis=2)
    gu = f["L0_ffn_w_up_gate"].reshape(E, KT, P, 2 * I).transpose(0, 2, 1, 3).reshape(E, P, KT * 2 * I)
    dn = np.pad(f["L0_ffn_w_down"], ((0, 0), (0, IT * P - I), (0, 0)))
    dn = dn.reshape(E, IT, P, D).transpose(0, 2, 1, 3).reshape(E, P, IT * D)
    w_expert = np.concatenate([gu, dn], axis=2)
    arrays = {
        "x": f["x"],
        "kv_t": np.ascontiguousarray(kv_t.reshape(NG, P, 2, 2 * S)),
        "kv_n": np.ascontiguousarray(ctxt.transpose(0, 2, 1, 3)),
        "gates": np.ascontiguousarray(np.broadcast_to(np.concatenate([f["g_xattn"], f["g_ffn"]]), (P, 2))),
        "Wq": f["L0_xattn_Wq"],
        "w_qk": np.ascontiguousarray(f["L0_xattn_w_kc_q"].transpose(2, 0, 1).reshape(DQ, H * P)),
        "W_qr": np.ascontiguousarray(f["L0_xattn_W_qr"].transpose(1, 0, 2).reshape(DQ, H * R)),
        "W_kr": np.ascontiguousarray(f["L0_xattn_W_kr"].transpose(1, 0, 2).reshape(P, H * R)),
        "w_kv": f["L0_xattn_w_kc_kv"],
        "Wo_t": np.ascontiguousarray(f["L0_xattn_Wo"].T),
        "router": f["L0_ffn_router"],
        "tables": np.concatenate([cos.T, sin.T, cos, sin], axis=1).astype(np.float32),
        "ident": np.eye(P, dtype=np.float32),
        "w_shared": w_shared,
        "w_expert": w_expert,
        "route_const": np.concatenate([np.triu(np.ones((P, P)), 1), np.ones((P, P)),
                                       np.broadcast_to(E - np.arange(E), (P, E))], axis=1).astype(np.float32),
        "token_ids": (np.arange(NB)[None, :] * P + np.arange(P)[:, None]).astype(np.int32),
    }
    args = [nc.dram_tensor(k, a.shape, mybir.dt.from_np(a.dtype), kind="ExternalInput").ap()
            for k, a in arrays.items()]
    out = nc.dram_tensor("result", (NB, S, D), F32, kind="ExternalOutput").ap()
    build(nc, *args, out)
    r = run(nc, [arrays], core_ids=[0])
    return r.results[0]["result"]
```
